# Optimizing a Trainium2 kernel written in Bass

```python
import numpy as np
import jax
import jax.numpy as jnp

def _softmax(x, axis=-1):
    return jax.nn.softmax(x, axis=axis)

def _gelu(x):
    return jax.nn.gelu(x, approximate=True)

def _silu(x):
    return jax.nn.silu(x)

def _sigmoid(x):
    return jax.nn.sigmoid(x)

def _layernorm(x, axis=-1, eps=1e-05):
    m = jnp.mean(x, axis=axis, keepdims=True)
    v = jnp.var(x, axis=axis, keepdims=True)
    return (x - m) / jnp.sqrt(v + eps)

def _scatter_add(tgt, idx, src, axis=0):
    return tgt.at[idx].add(src)

def _segment_sum(src, seg, n):
    return jax.ops.segment_sum(src, seg, n)
kernel_name = 'mk_macaron_d1_jaxref_r8_852e16'

def setup_inputs(seed: int=0):
    np.random.seed(seed)
    _w = jnp.asarray

    def _L0_attn_setup():
        import jax, jax.numpy as jnp
        import numpy as np
        N_HEAD = 16
        key = jax.random.key(seed)
        ks = jax.random.split(key, 9)
        H = 256

        def w(k, shape, scale=0.02):
            return jax.random.normal(k, shape, dtype=jnp.float32) * scale
        return {'h': jax.random.normal(ks[0], (4, 256, H), dtype=jnp.float32), 'Wq': w(ks[1], (H, H)), 'bq': w(ks[2], (H,)), 'Wk': w(ks[3], (H, H)), 'bk': w(ks[4], (H,)), 'Wv': w(ks[5], (H, H)), 'bv': w(ks[6], (H,)), 'Wo': w(ks[7], (H, H)), 'bo': w(ks[8], (H,))}
    _L0_attn_in = _L0_attn_setup()

    def _L0_ffn_setup():
        import jax, jax.numpy as jnp
        import numpy as np
        BLOCK_SIZE = 32
        HIDDEN_SIZE = 256
        MLP_DIM = 2048
        NVFP4_LUT = jnp.array([0.0, 0.5, 1.0, 1.5, 2.0, 3.0, 4.0, 6.0, 0.0, -0.5, -1.0, -1.5, -2.0, -3.0, -4.0, -6.0], dtype=jnp.float32)

        def dequant_nvfp4(W_packed, scales, block=BLOCK_SIZE):
            N = W_packed.shape[0]
            low = W_packed & 15
            high = W_packed >> 4 & 15
            idx = jnp.stack([low, high], axis=-1).reshape(N, -1)
            vals = NVFP4_LUT[idx]
            K = vals.shape[1]
            vals = vals.reshape(N, K // block, block) * scales[:, :, None]
            return vals.reshape(N, K)
        key = jax.random.key(seed)
        ks = jax.random.split(key, 7)
        x = jax.random.normal(ks[0], (4, 32, HIDDEN_SIZE), dtype=jnp.float32)
        gate_W_packed = jax.random.randint(ks[1], (MLP_DIM, HIDDEN_SIZE // 2), 0, 32, dtype=jnp.int32)
        gate_scales = jax.random.uniform(ks[2], (MLP_DIM, HIDDEN_SIZE // BLOCK_SIZE), dtype=jnp.float32) * 0.1 + 0.001
        up_W_packed = jax.random.randint(ks[3], (MLP_DIM, HIDDEN_SIZE // 2), 0, 32, dtype=jnp.int32)
        up_scales = jax.random.uniform(ks[4], (MLP_DIM, HIDDEN_SIZE // BLOCK_SIZE), dtype=jnp.float32) * 0.1 + 0.001
        down_W_packed = jax.random.randint(ks[5], (HIDDEN_SIZE, MLP_DIM // 2), 0, 32, dtype=jnp.int32)
        down_scales = jax.random.uniform(ks[6], (HIDDEN_SIZE, MLP_DIM // BLOCK_SIZE), dtype=jnp.float32) * 0.1 + 0.001
        return {'x': x, 'gate_W_packed': gate_W_packed, 'gate_scales': gate_scales, 'up_W_packed': up_W_packed, 'up_scales': up_scales, 'down_W_packed': down_W_packed, 'down_scales': down_scales}
    _L0_ffn_in = _L0_ffn_setup()
    _d = {'L0_attn_h': _L0_attn_in['h'], 'L0_attn_Wq': _L0_attn_in['Wq'], 'L0_attn_bq': _L0_attn_in['bq'], 'L0_attn_Wk': _L0_attn_in['Wk'], 'L0_attn_bk': _L0_attn_in['bk'], 'L0_attn_Wv': _L0_attn_in['Wv'], 'L0_attn_bv': _L0_attn_in['bv'], 'L0_attn_Wo': _L0_attn_in['Wo'], 'L0_attn_bo': _L0_attn_in['bo'], 'L0_ffn_gate_W_packed': _L0_ffn_in['gate_W_packed'], 'L0_ffn_gate_scales': _L0_ffn_in['gate_scales'], 'L0_ffn_up_W_packed': _L0_ffn_in['up_W_packed'], 'L0_ffn_up_scales': _L0_ffn_in['up_scales'], 'L0_ffn_down_W_packed': _L0_ffn_in['down_W_packed'], 'L0_ffn_down_scales': _L0_ffn_in['down_scales']}
    _x0 = _d['L0_attn_h']
    _d['L0_attn_h'] = jax.random.normal(jax.random.fold_in(jax.random.key(seed), 1), (1, 2048, 256), dtype=_x0.dtype)
    del _x0
    return _d

def reference(L0_attn_h, L0_attn_Wq, L0_attn_bq, L0_attn_Wk, L0_attn_bk, L0_attn_Wv, L0_attn_bv, L0_attn_Wo, L0_attn_bo, L0_ffn_gate_W_packed, L0_ffn_gate_scales, L0_ffn_up_W_packed, L0_ffn_up_scales, L0_ffn_down_W_packed, L0_ffn_down_scales):

    def _L0_attn_ref(h, Wq, bq, Wk, bk, Wv, bv, Wo, bo):
        import jax, jax.numpy as jnp
        import numpy as np
        N_HEAD = 16
        B, S, H = h.shape
        nh = N_HEAD
        hd = H // nh
        q = (h @ Wq.T + bq).reshape(B, S, nh, hd)
        k = (h @ Wk.T + bk).reshape(B, S, nh, hd)
        v = (h @ Wv.T + bv).reshape(B, S, nh, hd)
        scale = 1.0 / jnp.sqrt(jnp.float32(hd))
        scores = jnp.einsum('bqhd,bkhd->bhqk', q, k) * scale
        causal = jnp.tril(jnp.ones((S, S), dtype=bool))
        scores = jnp.where(causal, scores, jnp.finfo(scores.dtype).min)
        attn = jax.nn.softmax(scores, axis=-1)
        o = jnp.einsum('bhqk,bkhd->bqhd', attn, v).reshape(B, S, H)
        return o @ Wo.T + bo

    def _L0_ffn_ref(x, gate_W_packed, gate_scales, up_W_packed, up_scales, down_W_packed, down_scales):
        import jax, jax.numpy as jnp
        import numpy as np
        BLOCK_SIZE = 32
        HIDDEN_SIZE = 256
        MLP_DIM = 2048
        NVFP4_LUT = jnp.array([0.0, 0.5, 1.0, 1.5, 2.0, 3.0, 4.0, 6.0, 0.0, -0.5, -1.0, -1.5, -2.0, -3.0, -4.0, -6.0], dtype=jnp.float32)

        def dequant_nvfp4(W_packed, scales, block=BLOCK_SIZE):
            N = W_packed.shape[0]
            low = W_packed & 15
            high = W_packed >> 4 & 15
            idx = jnp.stack([low, high], axis=-1).reshape(N, -1)
            vals = NVFP4_LUT[idx]
            K = vals.shape[1]
            vals = vals.reshape(N, K // block, block) * scales[:, :, None]
            return vals.reshape(N, K)
        B, S, H = x.shape
        xt = x.reshape(B * S, H)
        Wg = dequant_nvfp4(gate_W_packed, gate_scales)
        Wu = dequant_nvfp4(up_W_packed, up_scales)
        Wd = dequant_nvfp4(down_W_packed, down_scales)
        gate = jnp.einsum('th,nh->tn', xt, Wg)
        up = jnp.einsum('th,nh->tn', xt, Wu)
        gelu = jnp.tanh(0.7978845608028654 * (gate + 0.044715 * gate ** 3)) * gate * 0.5 + gate * 0.5
        inter = gelu * up
        out = jnp.einsum('tn,hn->th', inter, Wd)
        return out.reshape(B, S, H)
    x = L0_attn_h
    x = x + 0.5 * _L0_ffn_ref(_layernorm(x, axis=-1), L0_ffn_gate_W_packed, L0_ffn_gate_scales, L0_ffn_up_W_packed, L0_ffn_up_scales, L0_ffn_down_W_packed, L0_ffn_down_scales)
    x = x + _L0_attn_ref(_layernorm(x, axis=-1), L0_attn_Wq, L0_attn_bq, L0_attn_Wk, L0_attn_bk, L0_attn_Wv, L0_attn_bv, L0_attn_Wo, L0_attn_bo)
    x = x + 0.5 * _L0_ffn_ref(_layernorm(x, axis=-1), L0_ffn_gate_W_packed, L0_ffn_gate_scales, L0_ffn_up_W_packed, L0_ffn_up_scales, L0_ffn_down_W_packed, L0_ffn_down_scales)
    return x

_drawn_inputs = setup_inputs


def setup_inputs(seed=0):
    import zlib

    import numpy as np

    out = dict(_drawn_inputs(seed))
    spreads = {}
    factors = {'L0_attn_Wq': 8.0,
     'L0_attn_bq': 8.0,
     'L0_attn_Wk': 8.0,
     'L0_attn_bk': 64.0,
     'L0_attn_Wv': 8.0,
     'L0_attn_bv': 8.0,
     'L0_attn_Wo': 8.0,
     'L0_attn_bo': 23.12}
    for name, (base, spread) in spreads.items():
        noise = np.random.default_rng([zlib.crc32(name.encode()), seed]).standard_normal(out[name].shape)
        drawn = base * np.exp(spread * noise) if base else spread * noise
        out[name] = jnp.asarray(drawn.astype(out[name].dtype))
    for name, factor in factors.items():
        out[name] = (out[name] * factor).astype(out[name].dtype)
    return out
```

```python
from contextlib import ExitStack

import concourse.bass as bass
from concourse import mybir

F32 = mybir.dt.float32
F32R = mybir.dt.float32r
BF16 = mybir.dt.bfloat16
I32 = mybir.dt.int32
U8 = mybir.dt.uint8
U16 = mybir.dt.uint16
ALU = mybir.AluOpType
ACT = mybir.ActivationFunctionType
AX = mybir.AxisListType

P = 128
T, H, F = 2048, 256, 2048
NH = 16
HD = H // NH
EPS = 1e-5
TT = T // P
BT = 512
NB = T // BT
SUB = BT // P
PL = 2
NQ = F // P
GT = 4
NG = NQ // GT
BLK = 16
GELU_C, GELU_A = 0.7978845608028654, 0.044715
PASSES = ((0, 0), (0, 1), (1, 0))
MASKED = -1e30
CREDIT = 2
START = -3e38

NPAIR = NH // 2
HALF = 64
NKB = T // P
KR = 3 * HD
SB = 3
SBANKS = 3
PRING = 8
VW = 34


def build_program(nc, h, Wq, bq, Wk, bk, Wv, bv, Wo, bo, gW, gS, uW, uS, dW, dS, out):
    nc.disable_value_cache = True
    outer = ExitStack()

    def tensors(stack, phase):
        return lambda name, shape, dt: stack.enter_context(nc.sbuf_tensor(f"{phase}_{name}", shape, dt))

    with outer:
        sb = tensors(outer, "all")
        x = sb("x", [P, TT, H], F32)
        heads = sb("heads", [P, TT, H], F32)
        w_hi = sb("w_hi", [P, 3 * NG, PL, GT * P], F32R)
        w_lo = sb("w_lo", [P, 3 * NG, PL, GT * P], F32R)
        w_part = (w_hi, w_lo)
        ident = sb("ident", [P, P], F32)
        stats = sb("stats", [P, TT, 6], F32)
        mean_var = sb("mean_var", [P, TT, 2], F32)
        var_eps = sb("var_eps", [P, TT], F32)
        deviation = sb("deviation", [P, TT], F32)
        rstd = sb("rstd", [P, TT], F32)
        psum = outer.enter_context(nc.psum_tensor("psum", [P, 8, BT], F32))
        qk_dram = nc.dram_tensor("qk_parts", (4, H, T), F32, kind="Internal").ap()
        v_dram = nc.dram_tensor("v_rows", (NPAIR, P, NKB, 2 * HD), F32, kind="Internal").ap()

        def as_f32(ap):
            return ap.bitcast(F32)

        def norm_vector(dve, s):
            for t in range(TT):
                nc.vector.bn_stats(stats[:, t, :], x[:, t, :]).then_inc(s["stats"], 1)
            for t in range(TT):
                dve.wait_ge(s["stats"], t + 1)
                last = nc.vector.bn_aggr(mean_var[:, t, :], stats[:, t, :])
            last.then_inc(s["aggr"], 1)
            dve.wait_ge(s["aggr"], 1)
            nc.vector.tensor_scalar(var_eps[:, :], mean_var[:, :, 1], EPS, None, ALU.add).then_inc(s["var"], 1)
            dve.wait_ge(s["std"], 1)
            nc.vector.reciprocal(rstd[:, :], deviation[:, :]).then_inc(s["rstd"], 1)
            dve.wait_ge(s["rstd"], 1)

        def norm_block(dve, s, b, xb):
            dve.wait_ge(s["turned"], b)
            for i in range(SUB):
                t = b * SUB + i
                last = nc.vector.tensor_scalar(xb[:, i, :], x[:, bass.ds(t, 1), :].rearrange("p o c -> p (o c)"),
                                               mean_var[:, bass.ds(t, 1), 0], rstd[:, bass.ds(t, 1)],
                                               ALU.subtract, ALU.mult)
            last.then_inc(s["xb"], 1)

        def norm_scalar(act, s):
            act.wait_ge(s["var"], 1)
            nc.scalar.activation(deviation[:, :], var_eps[:, :], ACT.Sqrt).then_inc(s["std"], 1)

        def turn_tensor(xb, bank):
            for pl in range(PL):
                for i in range(SUB):
                    last = nc.tensor.transpose(psum[:, bank + pl, i * P:(i + 1) * P],
                                               xb[:, i, pl::PL], ident[:, :])
            return last

        def dequantise(s):
            with ExitStack() as st:
                tb = tensors(st, "dequant")
                codes = tb("codes", [P, 3 * NG, GT, P], I32)
                scales = tb("scales", [P, 2, NG, GT, P // BLK], F32)
                d_scales = tb("d_scales", [P, 2, F // 32], F32)
                identb = tb("identb", [P, P], BF16)
                byte = tb("byte", [P, 2, GT * P], BF16)
                wide = tb("wide", [P, 2, GT, P], F32)
                turned = tb("turned", [P, 2, GT * P], U16)
                mag = tb("mag", [P, 2, PL, GT * P], U16)
                sign = tb("sign", [P, 2, PL, GT * P], U16)
                low = tb("low", [P, 2, PL, GT * P], BF16)
                weight = tb("weight", [P, 2, PL, GT * P], F32)
                NGR = 3 * NG

                def rows(w):
                    return w.rearrange("(c p two) j -> p c two j", p=P, two=2)

                with nc.Block() as block:
                    @block.sync
                    def _(sp):
                        for m, sc in ((0, gS), (1, uS)):
                            sp.dma_start(scales[:, m, :, :, :].rearrange("p g (c two) b -> p (g c) two b", two=2),
                                         rows(sc)).then_inc(s["scales"], 16)
                        sp.dma_start(d_scales[:, :, :], dS.rearrange("(hh p) b -> p hh b", p=P)).then_inc(s["scales"], 16)
                        for g in range(NG):
                            for m, w in ((0, gW), (1, uW)):
                                sp.dma_start(codes[:, 3 * g + m, :, :].rearrange("p (c two) j -> p c two j", two=2),
                                             rows(w)[:, 2 * g:2 * g + 2]).then_inc(s[f"codes{3 * g + m}"], 16)
                            for c in range(2):
                                sp.dma_start(codes[:, 3 * g + 2, 2 * c:2 * c + 2, :],
                                             dW[:, (2 * g + c) * P:(2 * g + c + 1) * P].rearrange("(hh p) j -> p hh j", p=P)
                                             ).then_inc(s[f"codes{3 * g + 2}"], 16)
                        for t in range(0, TT, 4):
                            sp.dma_start(x[:, t:t + 4, :], h[0, t * P:(t + 4) * P, :].rearrange("(t p) c -> p t c", p=P)
                                         ).then_inc(s["x"], 16)
                        sp.wait_ge(s["x"], 16 * (TT // 4))

                    @block.gpsimd
                    def _(pool):
                        nc.gpsimd.memset(ident[:, :], 0.0).then_inc(s["ident"], 1)
                        pool.wait_ge(s["ident"], 1)
                        nc.gpsimd.affine_select(out=ident[:, :], in_=ident[:, :], compare_op=ALU.not_equal, fill=1.0,
                                                base=0, pattern=[[-1, P]], channel_multiplier=1).then_inc(s["ident"], 1)
                        pool.wait_ge(s["ident"], 2)
                        nc.gpsimd.tensor_copy(identb[:, :], ident[:, :]).then_inc(s["ident"], 1)
                        pool.wait_ge(s["scales"], 48)
                        for n in range(NGR):
                            g, m = divmod(n, 3)
                            if n >= 2:
                                pool.wait_ge(s["turned_s"], n - 1)
                            for i in range(GT):
                                src = (scales[:, m, g, i, :] if m < 2 else
                                       d_scales[:, i % 2, 8 * (2 * g + i // 2):8 * (2 * g + i // 2) + 8])
                                last = nc.gpsimd.tensor_copy(wide[:, n % 2, i, :].rearrange("p (a b) -> p a b", b=BLK),
                                                             src.unsqueeze(2).broadcast_to([P, P // BLK, BLK]))
                            last.then_inc(s["wide"], 1)

                    @block.scalar
                    def _(act):
                        for n in range(NGR + 1):
                            if n < NGR:
                                act.wait_ge(s[f"codes{n}"], 16 if n % 3 < 2 else 32)
                                if n >= 2:
                                    act.wait_ge(s["turned_c"], n - 1)
                                nc.scalar.activation(byte[:, n % 2, :],
                                                     codes[:, n, :, :].rearrange("p a b -> p (a b)").bitcast(U8)[:, ::4],
                                                     ACT.Copy).then_inc(s["byte"], 1)
                                act.wait_ge(s["turned_c"], n + 1)
                                if n >= 2:
                                    act.wait_ge(s["weight"], n - 1)
                                nc.scalar.activation(turned[:, n % 2, :], psum[:, n % 2, 0:BT // 2].bitcast(BF16),
                                                     ACT.Copy).then_inc(s["turned"], 1)
                            if n >= 1:
                                act.wait_ge(s["weight"], n)
                                nc.scalar.activation(w_hi[:, n - 1, :, :], weight[:, (n - 1) % 2, :, :],
                                                     ACT.Copy).then_inc(s["w_hi"], 1)

                    @block.tensor
                    def _(pe):
                        pe.wait_ge(s["ident"], 3)
                        for n in range(NGR):
                            pe.wait_ge(s["byte"], n + 1)
                            if n >= 2:
                                pe.wait_ge(s["turned"], n - 1)
                            for i in range(GT):
                                last = nc.tensor.transpose(psum[:, n % 2, i * HALF:(i + 1) * HALF].bitcast(BF16),
                                                           byte[:, n % 2, i * P:(i + 1) * P], identb[:, :])
                            last.then_inc(s["turned_c"], 1)
                            pe.wait_ge(s["wide"], n + 1)
                            if n >= 2:
                                pe.wait_ge(s["weight"], n - 1)
                            for i in range(GT):
                                last = nc.tensor.transpose(psum[:, 2 + n % 2, i * P:(i + 1) * P], wide[:, n % 2, i, :],
                                                           ident[:, :])
                            last.then_inc(s["turned_s"], 1)

                    @block.vector
                    def _(dve):
                        def own(instruction, count):
                            instruction.then_inc(s["step"], 1)
                            dve.wait_ge(s["step"], count)

                        for n in range(NGR):
                            code, m, sg, lw = turned[:, n % 2, :], mag[:, n % 2], sign[:, n % 2], low[:, n % 2]
                            dve.wait_ge(s["turned"], n + 1)
                            nc.vector.tensor_scalar(m[:, 0, :], code, 0xF8, 6, ALU.bitwise_or, ALU.logical_shift_left)
                            nc.vector.tensor_scalar(sg[:, 0, :], code, 0x08, 12, ALU.bitwise_and, ALU.logical_shift_left)
                            nc.vector.tensor_scalar(sg[:, 1, :], code, 0x80, 8, ALU.bitwise_and, ALU.logical_shift_left)
                            own(nc.vector.tensor_scalar(m[:, 1, :], code, 0x70, 0xF80, ALU.bitwise_and, ALU.bitwise_or), 4 * n + 1)
                            own(nc.vector.tensor_scalar(m[:, 1, :], m[:, 1, :], 2, None, ALU.logical_shift_left), 4 * n + 2)
                            g8 = m.bitcast(BF16)
                            own(nc.vector.tensor_scalar(lw, g8, 8.0, -1.0, ALU.mult, ALU.add), 4 * n + 3)
                            nc.vector.scalar_tensor_tensor(g8, g8, 4.0, lw, ALU.mult, ALU.min).then_inc(s["value"], 1)
                            dve.wait_ge(s["value"], 2 * n + 1)
                            nc.vector.tensor_tensor(m, m, sg, ALU.bitwise_or).then_inc(s["value"], 1)
                            dve.wait_ge(s["value"], 2 * n + 2)
                            dve.wait_ge(s["turned_s"], n + 1)
                            if n >= 2:
                                dve.wait_ge(s["w_hi"], n - 1)
                            nc.vector.tensor_tensor(weight[:, n % 2], g8,
                                                    psum[:, 2 + n % 2, :].unsqueeze(1).broadcast_to([P, PL, BT]),
                                                    ALU.mult).then_inc(s["weight"], 1)
                            dve.wait_ge(s["w_hi"], n + 1)
                            own(nc.vector.tensor_tensor(w_lo[:, n], weight[:, n % 2], as_f32(w_hi[:, n]), ALU.subtract), 4 * n + 4)

        def ffn(phase, s, store):
            with ExitStack() as st:
                tb = tensors(st, phase)
                xb = tb("xb", [P, SUB, H], F32)
                xt = tb("xt", [P, 2, PL, BT], F32R)
                inner = tb("inner", [P, 2, 2, BT], F32R)
                arg = tb("arg", [P, 2, BT], F32)
                act_out = tb("act_out", [P, 2, BT], F32)
                ACC = 6

                with nc.Block() as block:
                    @block.tensor
                    def _(pe):
                        def turn(b):
                            pe.wait_ge(s["xb"], b + 1)
                            turn_tensor(xb, 4).then_inc(s["turned"], 1)

                        def gate_up(b, q):
                            pe.wait_ge(s["product"], b * NQ + q + 1)
                            g, o = q // GT, (q % GT) * P
                            for m in range(2):
                                n = 0
                                for pl in range(PL):
                                    for a, c in PASSES:
                                        last = nc.tensor.matmul(psum[:, 2 * m + q % 2, :],
                                                                w_part[a][:, 3 * g + m, pl, o:o + P], xt[:, c, pl, :],
                                                                start=(n == 0), stop=(n == 5))
                                        n += 1
                            last.then_inc(s["gu"], 1)

                        def down(b, q):
                            pe.wait_ge(s["inner_lo"], b * NQ + q + 1 + CREDIT)
                            if q == 0:
                                pe.wait_ge(s["added"], b)
                            c, pl = divmod(q, 2)
                            for i in range(SUB):
                                for n, (a, e) in enumerate(PASSES):
                                    last = nc.tensor.matmul(psum[:, ACC + i // 2, (i % 2) * H:(i % 2 + 1) * H],
                                                            inner[:, a, q % 2, i * P:(i + 1) * P],
                                                            w_part[e][:, 3 * (c // 2) + 2, pl, (c % 2) * H:(c % 2 + 1) * H],
                                                            start=(q == 0 and n == 0 and i % 2 == 0),
                                                            stop=(q == NQ - 1 and n == 2), skip_group_check=True)
                            last.then_inc(s["down"], 1)

                        def block_steps(b, more):
                            pe.wait_ge(s["xt_lo"], b + 1)
                            for q in range(NQ):
                                gate_up(b, q)
                                if q == NQ // 2 and more:
                                    turn(b + 1)
                                if q >= 2:
                                    down(b, q - 2)
                            down(b, NQ - 2)
                            down(b, NQ - 1)

                        turn(0)
                        with nc.tensor.Fori(0, NB - 1) as b:
                            block_steps(b, True)
                        block_steps(NB - 1, False)

                    @block.scalar
                    def _(act):
                        norm_scalar(act, s)

                        def split(b):
                            act.wait_ge(s["turned"], b + 1)
                            nc.scalar.activation(xt[:, 0, :, :], psum[:, 4:6, :], ACT.Copy).then_inc(s["xt_hi"], 1)

                        def block_steps(b, more):
                            for q in range(NQ):
                                n = b * NQ + q
                                u = q % 2
                                act.wait_ge(s["gu"], n + 1)
                                act.wait_ge(s["tanh"], n + 1)
                                nc.scalar.activation(arg[:, u, :], psum[:, u, :], ACT.Square).then_inc(s["square"], 1)
                                act.wait_ge(s["cubic"], n + 1)
                                act.wait_ge(s["inner_lo"], n + 1)
                                nc.scalar.activation(act_out[:, u, :], arg[:, u, :], ACT.Tanh,
                                                     scale=GELU_C).then_inc(s["tanh"], 1)
                                act.wait_ge(s["product"], n + 1 + CREDIT)
                                act.wait_ge(s["down"], n + 1)
                                nc.scalar.activation(inner[:, 0, u, :], act_out[:, u, :], ACT.Copy).then_inc(s["inner_hi"], 1)
                            if more:
                                split(b + 1)

                        act.sem_inc(s["tanh"], CREDIT)
                        split(0)
                        with nc.scalar.Fori(0, NB - 1) as b:
                            block_steps(b, True)
                        block_steps(NB - 1, False)

                    @block.vector
                    def _(dve):
                        dve.sem_inc(s["product"], CREDIT)
                        dve.sem_inc(s["inner_lo"], CREDIT)
                        norm_vector(dve, s)

                        def split(b):
                            dve.wait_ge(s["xt_hi"], b + 1)
                            nc.vector.tensor_tensor(xt[:, 1, :, :], psum[:, 4:6, :], as_f32(xt[:, 0, :, :]),
                                                    ALU.subtract).then_inc(s["xt_lo"], 1)

                        def low_part(b, q):
                            u = q % 2
                            dve.wait_ge(s["inner_hi"], b * NQ + q + 1)
                            nc.vector.tensor_tensor(inner[:, 1, u, :], act_out[:, u, :], as_f32(inner[:, 0, u, :]),
                                                    ALU.subtract).then_inc(s["inner_lo"], 1)

                        def block_steps(b, more):
                            for q in range(NQ):
                                n = b * NQ + q
                                u = q % 2
                                dve.wait_ge(s["square"], n + 1)
                                nc.vector.tensor_scalar(arg[:, u, :], arg[:, u, :], GELU_A, 1.0, ALU.mult,
                                                        ALU.add).then_inc(s["quadratic"], 1)
                                dve.wait_ge(s["quadratic"], n + 1)
                                nc.vector.tensor_tensor(arg[:, u, :], arg[:, u, :], psum[:, u, :],
                                                        ALU.mult).then_inc(s["cubic"], 1)
                                if q >= 1:
                                    low_part(b, q - 1)
                                if q == NQ // 2 - 2 and more:
                                    norm_block(dve, s, b + 1, xb)
                                dve.wait_ge(s["tanh"], n + 1 + CREDIT)
                                nc.vector.scalar_tensor_tensor(act_out[:, u, :], act_out[:, u, :], 1.0, psum[:, u, :],
                                                               ALU.add, ALU.mult).then_inc(s["gelu"], 1)
                                dve.wait_ge(s["gelu"], n + 1)
                                nc.vector.scalar_tensor_tensor(act_out[:, u, :], act_out[:, u, :], 0.5, psum[:, 2 + u, :],
                                                               ALU.mult, ALU.mult).then_inc(s["product"], 1)
                            if more:
                                split(b + 1)
                            low_part(b, NQ - 1)
                            dve.wait_ge(s["down"], (b + 1) * NQ + CREDIT)
                            for j in range(2):
                                dst = x[:, bass.ds(b * SUB + 2 * j, 2), :].rearrange("p a c -> p (a c)")
                                last = nc.vector.scalar_tensor_tensor(dst, psum[:, ACC + j, :], 0.5, dst, ALU.mult, ALU.add)
                            last.then_inc(s["added"], 1)

                        norm_block(dve, s, 0, xb)
                        split(0)
                        with nc.vector.Fori(0, NB - 1) as b:
                            block_steps(b, True)
                        block_steps(NB - 1, False)

                    @block.gpsimd
                    def _(pool):
                        pool.sem_inc(s["down"], CREDIT)

                    @block.sync
                    def _(sp):
                        if store:
                            with nc.sync.Fori(0, NB) as b:
                                sp.wait_ge(s["added"], b + 1)
                                sp.dma_start(out[0, bass.ds(b * BT, BT), :].rearrange("(t p) c -> p t c", p=P),
                                             x[:, bass.ds(b * SUB, SUB), :]).then_inc(s["stored"], 16)
                            sp.wait_ge(s["stored"], 16 * NB)

        def qkv(s):
            with ExitStack() as st:
                tb = tensors(st, "qkv")
                raw = tb("raw", [P, 3, 2, H], F32)
                wt = tb("wt", [P, 2, 3, PL, H], F32R)
                wfull = tb("wfull", [P, 3, PL, H], F32)
                bias = tb("bias", [P, 2, 2], F32)
                bias_v = tb("bias_v", [P, H], F32)
                xb = tb("xb", [P, SUB, H], F32)
                xt = tb("xt", [P, 2, PL, BT], F32R)
                full = tb("full", [P, 2, BT], F32)
                parts = tb("parts", [P, 2, 2, BT], F32R)
                rows_v = tb("rows_v", [P, 2, H], F32)
                bias_q = tb("bias_q", [P, 2], F32)
                SCALE = HD ** -0.5
                NU = 4

                with nc.Block() as block:
                    @block.sync
                    def _(sp):
                        for m, w in enumerate((Wq, Wk, Wv)):
                            sp.dma_start(raw[:, m, :, :], w.rearrange("(hh p) c -> p hh c", p=P)).then_inc(s["loaded"], 16)
                        for m, b_ in enumerate((bq, bk)):
                            sp.dma_start(bias[:, m, :], b_.rearrange("(hh p) -> p hh", p=P),
                                         allow_slow_non_contiguous=True).then_inc(s["loaded"], 16)
                        sp.dma_start(bias_v[:, :], bv.rearrange("(o c) -> o c", o=1).broadcast_to([P, H])).then_inc(s["loaded"], 16)
                        with nc.sync.Fori(0, NB) as b:
                            for u in range(NU):
                                kind, half = divmod(u, 2)
                                sp.wait_ge(s["part_lo"], b * NU + u + 1 + CREDIT)
                                sp.dma_start(qk_dram[2 * kind:2 * kind + 2, half * P:(half + 1) * P, bass.ds(b * BT, BT)]
                                             .rearrange("a p t -> p a t"), as_f32(parts[:, u % 2, :, :])).then_inc(s[f"part_out{u % 2}"], 16)
                            for i in range(SUB):
                                sp.wait_ge(s["v"], b * SUB + i + 1 + CREDIT)
                                sp.dma_start(v_dram[:, :, bass.ds(b * SUB + i, 1), :].rearrange("r p o c -> p r (o c)"),
                                             rows_v[:, i % 2, :].rearrange("p (r c) -> p r c", c=2 * HD)).then_inc(s[f"v_out{i % 2}"], 16)
                        for u in range(2):
                            sp.wait_ge(s[f"part_out{u}"], 16 + 16 * NB * NU // 2)
                            sp.wait_ge(s[f"v_out{u}"], 16 + 16 * TT // 2)

                    @block.tensor
                    def _(pe):
                        pe.wait_ge(s["loaded"], 96)
                        for m in range(3):
                            if m == 2:
                                pe.wait_ge(s["wt_lo"], 1)
                            for pl in range(PL):
                                for hh in range(2):
                                    last = nc.tensor.transpose(psum[:, 2 * (m % 2) + pl, hh * P:(hh + 1) * P],
                                                               raw[:, m, hh, pl::PL], ident[:, :])
                            last.then_inc(s["wt"], 1)

                        pe.wait_ge(s["wt_lo"], 3)
                        with nc.tensor.Fori(0, NB) as b:
                            pe.wait_ge(s["xb"], b + 1)
                            turn_tensor(xb, 4).then_inc(s["turned"], 1)
                            pe.wait_ge(s["xt_lo"], b + 1)
                            for u in range(NU):
                                kind, half = divmod(u, 2)
                                pe.wait_ge(s["full"], b * NU + u + 1)
                                n = 0
                                for pl in range(PL):
                                    for a, c in PASSES:
                                        last = nc.tensor.matmul(psum[:, u % 2, :], wt[:, a, kind, pl, half * P:(half + 1) * P],
                                                                xt[:, c, pl, :], start=(n == 0), stop=(n == 5))
                                        n += 1
                                last.then_inc(s["unit"], 1)
                            for i in range(SUB):
                                pe.wait_ge(s["v"], b * SUB + i + 1)
                                n = 0
                                for pl in range(PL):
                                    for a, c in PASSES:
                                        last = nc.tensor.matmul(psum[:, 2 + i % 2, 0:H], xt[:, a, pl, i * P:(i + 1) * P],
                                                                wt[:, c, 2, pl, :], start=(n == 0), stop=(n == 5))
                                        n += 1
                                last.then_inc(s["v_sum"], 1)

                    @block.scalar
                    def _(act):
                        norm_scalar(act, s)
                        act.wait_ge(s["loaded"], 96)
                        nc.scalar.activation(bias_q[:, :], bias[:, 0, :], ACT.Copy, scale=SCALE).then_inc(s["bias_q"], 1)
                        for m in range(3):
                            act.wait_ge(s["wt"], m + 1)
                            nc.scalar.activation(wfull[:, m, :, :], psum[:, 2 * (m % 2):2 * (m % 2) + 2, 0:H], ACT.Copy).then_inc(s["wfull"], 1)
                        act.sem_inc(s["full"], CREDIT)
                        with nc.scalar.Fori(0, NB) as b:
                            act.wait_ge(s["turned"], b + 1)
                            act.wait_ge(s["v_sum"], b * SUB)
                            nc.scalar.activation(xt[:, 0, :, :], psum[:, 4:6, :], ACT.Copy).then_inc(s["xt_hi"], 1)
                            for u in range(NU):
                                kind, half = divmod(u, 2)
                                act.wait_ge(s["unit"], b * NU + u + 1)
                                act.wait_ge(s["part_lo"], b * NU + u + 1)
                                act.wait_ge(s["bias_q"], 1)
                                nc.scalar.activation(full[:, u % 2, :], psum[:, u % 2, :], ACT.Identity,
                                                     scale=SCALE if kind == 0 else 1.0,
                                                     bias=bias_q[:, half:half + 1] if kind == 0 else bias[:, 1, half:half + 1]
                                                     ).then_inc(s["full"], 1)

                    @block.vector
                    def _(dve):
                        dve.sem_inc(s["v"], CREDIT)
                        dve.sem_inc(s["part_lo"], CREDIT)
                        norm_vector(dve, s)
                        for m in range(3):
                            dve.wait_ge(s["wfull"], m + 1)
                            nc.vector.tensor_copy(wt[:, 0, m, :, :], wfull[:, m, :, :]).then_inc(s["wt_hi"], 1)
                            dve.wait_ge(s["wt_hi"], m + 1)
                            nc.vector.tensor_tensor(wt[:, 1, m, :, :], wfull[:, m, :, :], as_f32(wt[:, 0, m, :, :]),
                                                    ALU.subtract).then_inc(s["wt_lo"], 1)
                        with nc.vector.Fori(0, NB) as b:
                            norm_block(dve, s, b, xb)
                            dve.wait_ge(s["xt_hi"], b + 1)
                            nc.vector.tensor_tensor(xt[:, 1, :, :], psum[:, 4:6, :], as_f32(xt[:, 0, :, :]),
                                                    ALU.subtract).then_inc(s["xt_lo"], 1)
                            for u in range(NU):
                                dve.wait_ge(s["full"], b * NU + u + 1 + CREDIT)
                                dve.wait_ge(s[f"part_out{u % 2}"], (b * (NU // 2) + u // 2 + 1) * 16)
                                nc.vector.tensor_copy(parts[:, u % 2, 0, :], full[:, u % 2, :]).then_inc(s["part_hi"], 1)
                                dve.wait_ge(s["part_hi"], b * NU + u + 1)
                                nc.vector.tensor_tensor(parts[:, u % 2, 1, :], full[:, u % 2, :], as_f32(parts[:, u % 2, 0, :]),
                                                        ALU.subtract).then_inc(s["part_lo"], 1)
                            for i in range(SUB):
                                dve.wait_ge(s["v_sum"], b * SUB + i + 1)
                                dve.wait_ge(s[f"v_out{i % 2}"], (b * (SUB // 2) + i // 2 + 1) * 16)
                                nc.vector.tensor_tensor(rows_v[:, i % 2, :], psum[:, 2 + i % 2, 0:H], bias_v[:, :],
                                                        ALU.add).then_inc(s["v"], 1)

                    @block.gpsimd
                    def _(pool):
                        for u in range(2):
                            pool.sem_inc(s[f"part_out{u}"], 16)
                            pool.sem_inc(s[f"v_out{u}"], 16)

        def attention(s):
            steps = [(qt, kb) for qt in range(NB) for kb in range(0, SUB * (qt + 1), 2)]
            NS = len(steps)
            NT = 4 * NS
            chunks = [(i, c) for i in range(TT) for c in range(i // SUB + 1)]
            NM = 2 * len(chunks)
            LEAD = NS - 3
            quota = [len(chunks) * min(d + 1, LEAD) // LEAD for d in range(NS)]
            S0, M0, O0, X0 = 0, 3, 5, 7

            def first_query(qt, kb):
                at = max(0, P * (kb - SUB * qt))
                return 0 if (qt, kb) == (0, 1) else at

            masks = [(d, 2 * k + hd) for d, (qt, kb) in enumerate(steps) if kb >= SUB * qt for k in range(2) for hd in range(2)]
            NMASK = len(masks)

            with ExitStack() as st:
                tb = tensors(st, "attn")
                stack = tb("stack", [P, SB, 2, T], F32R)
                prob = tb("prob", [P, PRING, BT], F32)
                vals = tb("vals", [P, SB, NKB, VW], F32)
                o_sb = tb("o_sb", [P, 2, BT], F32)
                pick = tb("pick", [P, VW], F32)
                mask = tb("mask", [P, BT], BF16)
                junk = tb("junk", [P, BT], BF16)
                part_max = tb("part_max", [P, 2, TT, NB], F32)
                row_max = tb("row_max", [P, 2, TT], F32)
                max_r = tb("max_r", [P, 2, TT], F32R)
                max_parts = tb("max_parts", [P, 2, 2, TT], F32)
                max_rows = tb("max_rows", [HALF, P], F32)
                rden = tb("rden", [P, SUB, 2], F32)

                def alone(engine, s):
                    engine.sem_inc(s["passed"], 1)

                def q_of(b):
                    return stack[:, b, 0, :]

                def k_of(b):
                    return stack[:, b, 1, :]

                def loop(engine, body):
                    with engine.Fori(0, NPAIR // SB) as it:
                        for r in range(SB):
                            body(it * SB + r, it, r, True)
                    for r in range(NPAIR % SB):
                        it = NPAIR // SB
                        body(it * SB + r, it, r, r < NPAIR % SB - 1)

                def loaded(it, r):
                    return (it + r // SB + 1) * 13 * 16

                with nc.Block() as block:
                    @block.sync
                    def _(sp):
                        def load(p, b):
                            for hd in range(2):
                                base = HALF * hd
                                rows = bass.ds(p * 2 * HD + hd * HD, HD)
                                q, k = as_f32(q_of(b)), as_f32(k_of(b))
                                for j in range(2):
                                    sp.dma_start(q[base + j * HD:base + (j + 1) * HD, :], qk_dram[0, rows, :]).then_inc(s[f"stack{b}"], 16)
                                    sp.dma_start(k[base + j * HD:base + (j + 1) * HD, :], qk_dram[2 + j, rows, :]).then_inc(s[f"stack{b}"], 16)
                                sp.dma_start(q[base + 2 * HD:base + KR, :], qk_dram[1, rows, :]).then_inc(s[f"stack{b}"], 16)
                                sp.dma_start(k[base + 2 * HD:base + KR, :], qk_dram[2, rows, :]).then_inc(s[f"stack{b}"], 16)
                            sp.dma_start(vals[:, b, :, 1:1 + 2 * HD], v_dram[bass.ds(p, 1), :, :, :].rearrange("o p k c -> p (o k) c")
                                         ).then_inc(s[f"stack{b}"], 16)

                        def max_row(p, b):
                            sp.wait_ge(s["max_rows"], p + 1)
                            for hd in range(2):
                                r = HALF * hd + KR
                                sp.dma_start(as_f32(q_of(b))[r:r + 2, :], max_rows[2 * hd * TT:2 * (hd + 1) * TT, :]
                                             ).then_inc(s["max_loaded"], 16)

                        sp.wait_ge(s["ones"], 2 * SB + 2)
                        load(0, 0)
                        load(1, 1)
                        max_row(0, 0)

                        def pair(p, it, r, more):
                            if not isinstance(p, int):
                                sp.wait_ge(s["scored"], p * NT)
                                sp.wait_ge(s["weighted"], p * NS + CREDIT)
                                load(p + 2, (r + 2) % SB)
                            if more:
                                max_row(p + 1, (r + 1) % SB)

                        loop(nc.sync, pair)

                    @block.gpsimd
                    def _(pool):
                        for b in range(SB):
                            for base in (0, HALF):
                                nc.gpsimd.memset(as_f32(stack[base + 32:base + HALF, b, 1, :]), -1.0).then_inc(s["ones"], 1)
                        pool.wait_ge(s["ones"], 2 * SB)
                        nc.gpsimd.memset(vals[:, :, :, 0:1], 1.0).then_inc(s["ones"], 1)
                        nc.gpsimd.memset(vals[:, :, :, VW - 1:VW], 1.0).then_inc(s["ones"], 1)
                        nc.gpsimd.memset(part_max[:, :, :, :], START).then_inc(s["mask"], 1)
                        nc.gpsimd.memset(mask[:, :], 0.0).then_inc(s["mask"], 1)
                        nc.gpsimd.memset(pick[:, :], 0.0).then_inc(s["mask"], 1)
                        pool.wait_ge(s["mask"], 3)
                        nc.gpsimd.affine_select(out=mask[:, BT - P:BT], in_=mask[:, BT - P:BT], compare_op=ALU.is_ge, fill=MASKED,
                                                base=0, pattern=[[-1, P]], channel_multiplier=1).then_inc(s["mask"], 1)
                        n = 4
                        for hd, (first, den) in enumerate(((1, 0), (HD - 1, 2 * HD - 1))):
                            for k in range(2):
                                row = 32 * (2 * hd + k)
                                for cols, r in ((pick[:, hd * HD:(hd + 1) * HD], row + first), (pick[:, 2 * HD + hd:2 * HD + hd + 1], row + den)):
                                    pool.wait_ge(s["mask"], n)
                                    nc.gpsimd.affine_select(out=cols, in_=cols, compare_op=ALU.not_equal, fill=1.0, base=-r,
                                                            pattern=[[-1, cols.shape[1]]], channel_multiplier=1).then_inc(s["mask"], 1)
                                    n += 1

                        def pair(p, it, r, more):
                            for n, (d, j) in enumerate(masks):
                                qt, kb = steps[d]
                                kb += j // 2
                                at = first_query(qt, kb)
                                wide = 2 * P if (qt, kb) == (0, 1) else P
                                t = prob[:, (4 * d + j) % PRING, at:at + wide]
                                pool.wait_ge(s["exp"], p * NT + 4 * d + j + 1 + SBANKS)
                                alone(pool, s)
                                nc.gpsimd.affine_select(out=t, in_=t, compare_op=ALU.is_ge, fill=0.0, base=P - wide,
                                                        pattern=[[1, wide]], channel_multiplier=-1).then_inc(s["masked"], 1)

                        loop(nc.gpsimd, pair)

                    @block.tensor
                    def _(pe):
                        pe.wait_ge(s["mask"], 12)

                        def score(p, b, d, j):
                            k, hd = divmod(j, 2)
                            qt, kb = steps[d]
                            at = first_query(qt, kb + k)
                            n = 4 * d + j
                            rows = slice(HALF * hd, HALF * hd + KR + 2)
                            pe.wait_ge(s["exp"], p * NT + n + 1)
                            nc.tensor.matmul(psum[:, S0 + (b * NT + n) % SBANKS, at:BT], k_of(b)[rows, (kb + k) * P:(kb + k + 1) * P],
                                             q_of(b)[rows, qt * BT + at:(qt + 1) * BT], start=True, stop=True).then_inc(s["scored"], 1)

                        def maxima(p, b, m):
                            i, c = chunks[m]
                            cols = BT if c < i // SUB else P * (i % SUB + 1)
                            for hd in range(2):
                                rows = slice(HALF * hd, HALF * hd + KR)
                                pe.wait_ge(s["max_read"], p * NM + 2 * m + hd + 1)
                                nc.tensor.matmul(psum[:, M0 + hd, 0:cols], q_of(b)[rows, i * P:(i + 1) * P],
                                                 k_of(b)[rows, c * BT:c * BT + cols], start=True, stop=True).then_inc(s["max_scored"], 1)

                        def turn_max(p):
                            pe.wait_ge(s["max_parts"], p + 1)
                            if not (isinstance(p, int) and p == 0):
                                pe.wait_ge(s["normed"], (p - 1) * NB + NB - 1)
                            alone(pe, s)
                            nc.tensor.transpose(psum[0:HALF, X0, 0:P], max_parts[:, :, :, :].rearrange("p a b c -> p (a b c)"),
                                                ident[:, :]).then_inc(s["max_turned"], 1)

                        def weigh(p, b, d):
                            qt, kb = steps[d]
                            pe.wait_ge(s["exp"], p * NT + 4 * d + 4 + SBANKS)
                            done = sum(1 for e, _ in masks if e <= d)
                            if kb >= SUB * qt:
                                pe.wait_ge(s["masked"], p * NMASK + done)
                            if kb == 0:
                                pe.wait_ge(s["o_copied"], p * NB + qt + 1)
                            for hd in range(2):
                                for k in range(2):
                                    at = first_query(qt, kb + k)
                                    r = 32 * (2 * hd + k)
                                    last = nc.tensor.matmul(psum[r:r + 32, O0 + qt % 2, at:BT], vals[:, b, kb + k, 2 * hd:2 * hd + 32],
                                                            prob[:, (4 * d + 2 * k + hd) % PRING, at:BT], start=(kb == 0),
                                                            stop=(kb == SUB * (qt + 1) - 2), skip_group_check=True)
                            last.then_inc(s["weighted"], 1)

                        def gather(p, qt):
                            pe.wait_ge(s["o_copied"], p * NB + qt + 1 + CREDIT)
                            pe.wait_ge(s["max_rows"], p + 1)
                            if qt == NB - 1 and not (isinstance(p, int) and p == NPAIR - 1):
                                pe.wait_ge(s["max_rows"], p + 2)
                            if not (isinstance(p, int) and p == 0 and qt == 0):
                                pe.wait_ge(s["normed"], p * NB + qt)
                            for i in range(SUB):
                                last = nc.tensor.matmul(psum[:, X0, i * VW:(i + 1) * VW], o_sb[:, qt % 2, i * P:(i + 1) * P], pick[:, :],
                                                        start=True, stop=True)
                            last.then_inc(s["gathered"], 1)

                        def pair(p, it, r, more):
                            nb = (r + 1) % SB
                            pe.wait_ge(s["max_loaded"], 32 * (p + 1))
                            if more:
                                pe.wait_ge(s[f"stack{nb}"], loaded(it, r + 1))
                            for d in range(NS):
                                before = quota[d - 1] if d else 0
                                middle = (before + quota[d]) // 2
                                for k, ms in enumerate((range(before, middle), range(middle, quota[d]))):
                                    score(p, r, d, 2 * k)
                                    score(p, r, d, 2 * k + 1)
                                    if more:
                                        for m in ms:
                                            maxima(p + 1, nb, m)
                                if d >= 1:
                                    weigh(p, r, d - 1)
                                if d >= 2 and steps[d - 1][0] != steps[d - 2][0]:
                                    gather(p, steps[d - 2][0])
                                if d == NS - 2 and more:
                                    turn_max(p + 1)
                            weigh(p, r, NS - 1)
                            gather(p, NB - 1)

                        pe.wait_ge(s["stack0"], loaded(0, 0))
                        for m in range(len(chunks)):
                            maxima(0, 0, m)
                        turn_max(0)
                        loop(nc.tensor, pair)

                    @block.scalar
                    def _(act):
                        def copy_max(p):
                            act.wait_ge(s["max_turned"], p + 1)
                            act.wait_ge(s["max_loaded"], 32 * p)
                            nc.scalar.activation(max_rows[:, :], psum[0:HALF, X0, 0:P], ACT.Copy).then_inc(s["max_rows"], 1)

                        def copy_out(p, qt):
                            act.wait_ge(s["weighted"], p * NS + sum(1 for e in steps if e[0] <= qt) + CREDIT)
                            act.wait_ge(s["gathered"], p * NB + qt + 1)
                            nc.scalar.activation(o_sb[:, qt % 2, :], psum[:, O0 + qt % 2, :], ACT.Copy).then_inc(s["o_copied"], 1)

                        def pair(p, it, r, more):
                            for d, (qt, kb) in enumerate(steps):
                                act.wait_ge(s["weighted"], p * NS + d + 1)
                                for j in range(4):
                                    at = first_query(qt, kb + j // 2)
                                    n = 4 * d + j
                                    act.wait_ge(s["scored"], p * NT + n + 1)
                                    nc.scalar.activation(prob[:, n % PRING, at:BT], psum[:, S0 + (r * NT + n) % SBANKS, at:BT],
                                                         ACT.Exp).then_inc(s["exp"], 1)
                                if d >= 1 and steps[d - 1][0] != qt:
                                    copy_out(p, qt - 1)
                                if d == NS - 2 and more:
                                    copy_max(p + 1)
                            copy_out(p, NB - 1)

                        act.sem_inc(s["exp"], SBANKS)
                        act.sem_inc(s["o_copied"], CREDIT)
                        act.wait_ge(s["max_turned"], 1)
                        nc.scalar.activation(max_rows[:, :], psum[0:HALF, X0, 0:P], ACT.Copy).then_inc(s["max_rows"], 1)
                        loop(nc.scalar, pair)

                    @block.vector
                    def _(dve):
                        def maxima(p, m):
                            i, c = chunks[m]
                            if m == 0 and not (isinstance(p, int) and p == 0):
                                dve.wait_ge(s["row_max"], p)
                            diagonal = [e for e in range(m) if chunks[e][1] == chunks[e][0] // SUB]
                            for hd in range(2):
                                dve.wait_ge(s["max_scored"], p * NM + 2 * m + hd + 1)
                                to = part_max[:, hd, i, c:c + 1]
                                if c < i // SUB:
                                    nc.vector.tensor_reduce(to, psum[:, M0 + hd, :], AX.X, ALU.max).then_inc(s["max_read"], 1)
                                else:
                                    cols = P * (i % SUB + 1)
    
                                    dve.wait_ge(s["max_read"], p * NM + (2 * m + hd if hd else 2 * diagonal[-1] + 2 if diagonal else 0) + CREDIT)
                                    alone(dve, s)
                                    nc.vector.tensor_tensor_reduce(out=junk[:, 0:cols], in0=psum[:, M0 + hd, 0:cols],
                                                                   in1=mask[:, BT - cols:BT], scale=1.0, scalar=START,
                                                                   op0=ALU.add, op1=ALU.max, accum_out=to).then_inc(s["max_read"], 1)

                        def split_max(p):
                            dve.wait_ge(s["max_read"], (p + 1) * NM + CREDIT)
                            if not (isinstance(p, int) and p == 0):
                                dve.wait_ge(s["max_turned"], p)
                            nc.vector.tensor_reduce(row_max[:, :, :], part_max[:, :, :, :], AX.X, ALU.max).then_inc(s["row_max"], 1)
                            dve.wait_ge(s["row_max"], p + 1)
                            nc.vector.tensor_copy(max_r[:, :, :], row_max[:, :, :]).then_inc(s["max_hi"], 1)
                            dve.wait_ge(s["max_hi"], p + 1)
                            nc.vector.tensor_copy(max_parts[:, :, 0, :], as_f32(max_r[:, :, :]))
                            nc.vector.tensor_tensor(max_parts[:, :, 1, :], row_max[:, :, :], as_f32(max_r[:, :, :]),
                                                    ALU.subtract).then_inc(s["max_parts"], 1)

                        def normalise(p, qt):
                            dve.wait_ge(s["gathered"], p * NB + qt + 1 + CREDIT)
                            got = psum[:, X0, 0:SUB * VW].rearrange("p (i c) -> p i c", c=VW)
                            dve.wait_ge(s["normed"], p * NB + qt)
                            nc.vector.reciprocal(rden[:, :, :], got[:, :, 2 * HD:]).then_inc(s["rden"], 1)
                            dve.wait_ge(s["rden"], p * NB + qt + 1)
                            nc.vector.tensor_tensor(heads[:, qt * SUB:(qt + 1) * SUB, bass.ds(p * 2 * HD, 2 * HD)].rearrange(
                                                        "p i (a c) -> p i a c", c=HD),
                                                    got[:, :, 0:2 * HD].rearrange("p i (a c) -> p i a c", c=HD),
                                                    rden[:, :, :].unsqueeze(3).broadcast_to([P, SUB, 2, HD]),
                                                    ALU.mult).then_inc(s["normed"], 1)

                        def pair(p, it, r, more):
                            for d in range(NS):
                                if more:
                                    for m in range(quota[d - 1] if d else 0, quota[d]):
                                        maxima(p + 1, m)
                                    if quota[d] == len(chunks) and (d == 0 or quota[d - 1] < len(chunks)):
                                        split_max(p + 1)
                                if d >= 2 and steps[d - 1][0] != steps[d - 2][0]:
                                    normalise(p, steps[d - 2][0])
                            normalise(p, NB - 1)

                        dve.sem_inc(s["max_read"], CREDIT)
                        dve.sem_inc(s["gathered"], CREDIT)
                        dve.sem_inc(s["weighted"], CREDIT)
                        dve.wait_ge(s["mask"], 12)
                        for m in range(len(chunks)):
                            maxima(0, m)
                        split_max(0)
                        loop(nc.vector, pair)

        def project(s):
            with ExitStack() as st:
                tb = tensors(st, "proj")
                raw = tb("raw_o", [P, 2, H], F32)
                wfull = tb("wfull_o", [P, PL, H], F32)
                wt = tb("wt_o", [P, 2, PL, H], F32R)
                bias = tb("bias_o", [P, H], F32)
                xb = tb("xb", [P, SUB, H], F32)
                ot = tb("ot", [P, 2, PL, BT], F32R)
                with nc.Block() as block:
                    @block.sync
                    def _(sp):
                        sp.dma_start(raw[:, :, :], Wo.rearrange("(hh p) c -> p hh c", p=P)).then_inc(s["loaded"], 16)
                        sp.dma_start(bias[:, :], bo.rearrange("(o c) -> o c", o=1).broadcast_to([P, H])).then_inc(s["loaded"], 16)

                    @block.tensor
                    def _(pe):
                        pe.wait_ge(s["loaded"], 32)
                        for pl in range(PL):
                            for hh in range(2):
                                last = nc.tensor.transpose(psum[:, pl, hh * P:(hh + 1) * P], raw[:, hh, pl::PL], ident[:, :])
                        last.then_inc(s["wt"], 1)
                        pe.wait_ge(s["wt_lo"], 1)
                        with nc.tensor.Fori(0, NB) as b:
                            pe.wait_ge(s["xb"], b + 1)
                            turn_tensor(xb, 4).then_inc(s["turned"], 1)
                            pe.wait_ge(s["ot_lo"], b + 1)
                            for i in range(SUB):
                                pe.wait_ge(s["added"], b * SUB + i + 1)
                                n = 0
                                for pl in range(PL):
                                    for a, c in PASSES:
                                        last = nc.tensor.matmul(psum[:, i, 0:H], ot[:, a, pl, i * P:(i + 1) * P],
                                                                wt[:, c, pl, :], start=(n == 0), stop=(n == 5))
                                        n += 1
                                last.then_inc(s["summed"], 1)

                    @block.scalar
                    def _(act):
                        act.wait_ge(s["wt"], 1)
                        nc.scalar.activation(wfull[:, :, :], psum[:, 0:2, 0:H], ACT.Copy).then_inc(s["wfull"], 1)
                        with nc.scalar.Fori(0, NB) as b:
                            act.wait_ge(s["turned"], b + 1)
                            act.wait_ge(s["summed"], b * SUB)
                            nc.scalar.activation(ot[:, 0, :, :], psum[:, 4:6, :], ACT.Copy).then_inc(s["ot_hi"], 1)

                    @block.vector
                    def _(dve):
                        dve.sem_inc(s["added"], SUB)
                        dve.wait_ge(s["loaded"], 32)
                        nc.vector.tensor_tensor(x[:, :, :], x[:, :, :], bias[:, :].unsqueeze(1).broadcast_to([P, TT, H]),
                                                ALU.add).then_inc(s["biased"], 1)
                        dve.wait_ge(s["wfull"], 1)
                        nc.vector.tensor_copy(wt[:, 0, :, :], wfull[:, :, :]).then_inc(s["wt_hi"], 1)
                        dve.wait_ge(s["wt_hi"], 1)
                        nc.vector.tensor_tensor(wt[:, 1, :, :], wfull[:, :, :], as_f32(wt[:, 0, :, :]), ALU.subtract).then_inc(s["wt_lo"], 1)
                        dve.wait_ge(s["biased"], 1)
                        with nc.vector.Fori(0, NB) as b:
                            dve.wait_ge(s["turned"], b)
                            nc.vector.tensor_copy(xb[:, :, :], heads[:, bass.ds(b * SUB, SUB), :]).then_inc(s["xb"], 1)
                            dve.wait_ge(s["ot_hi"], b + 1)
                            nc.vector.tensor_tensor(ot[:, 1, :, :], psum[:, 4:6, :], as_f32(ot[:, 0, :, :]),
                                                    ALU.subtract).then_inc(s["ot_lo"], 1)
                            for i in range(SUB):
                                dve.wait_ge(s["summed"], b * SUB + i + 1)
                                dst = x[:, bass.ds(b * SUB + i, 1), :].rearrange("p o c -> p (o c)")
                                nc.vector.tensor_tensor(dst, psum[:, i, 0:H], dst, ALU.add).then_inc(s["added"], 1)

        NORM = "stats aggr var std rstd xb "
        W_SEMS = "scales x ident turned_s wide turned_c byte turned weight w_hi step value " + " ".join(f"codes{n}" for n in range(3 * NG))
        F_SEMS = NORM + "turned gu product inner_lo down added xt_hi xt_lo tanh square cubic quadratic gelu inner_hi stored"
        Q_SEMS = NORM + ("loaded wt wfull wt_hi wt_lo turned xt_hi xt_lo full unit v_sum v bias_q part_hi part_lo "
                         "part_out0 part_out1 v_out0 v_out1")
        A_SEMS = ("stack0 stack1 stack2 max_rows max_loaded ones scored weighted mask exp masked max_read max_scored max_parts "
                  "passed normed max_turned o_copied gathered row_max max_hi rden")
        O_SEMS = "xb loaded wt wfull wt_hi wt_lo turned ot_hi ot_lo summed added biased"

        def named(phase, names):
            return {n: outer.enter_context(nc.semaphore(f"{phase}_{n}")) for n in names.split()}

        dequantise(named("dequant", W_SEMS))
        ffn("ffn1", named("ffn1", F_SEMS), False)
        qkv(named("qkv", Q_SEMS))
        attention(named("attn", A_SEMS))
        project(named("proj", O_SEMS))
        ffn("ffn2", named("ffn2", F_SEMS), True)


_INS = ["L0_attn_h", "L0_attn_Wq", "L0_attn_bq", "L0_attn_Wk", "L0_attn_bk", "L0_attn_Wv", "L0_attn_bv", "L0_attn_Wo",
        "L0_attn_bo", "L0_ffn_gate_W_packed", "L0_ffn_gate_scales", "L0_ffn_up_W_packed", "L0_ffn_up_scales",
        "L0_ffn_down_W_packed", "L0_ffn_down_scales"]


def kernel(**inputs):
    import numpy as _np
    import concourse.bacc as _bacc
    from concourse import mybir as _mybir
    from concourse.bass_utils import run_bass_kernel_spmd as _run

    nc = _bacc.Bacc("TRN2", target_bir_lowering=False, num_devices=1)
    arrays, args = {}, []
    for name in _INS:
        a = _np.ascontiguousarray(inputs[name])
        arrays[f"in_{name}"] = a
        args.append(nc.dram_tensor(f"in_{name}", a.shape, _mybir.dt.from_np(a.dtype), kind="ExternalInput").ap())
    args.append(nc.dram_tensor("out", (1, T, H), F32, kind="ExternalOutput").ap())
    build_program(nc, *args)
    r = _run(nc, [arrays], core_ids=[0])
    return r.results[0]["out"]
```

```python
from contextlib import ExitStack

import concourse.bass as bass
from concourse import mybir

F32 = mybir.dt.float32
F32R = mybir.dt.float32r
BF16 = mybir.dt.bfloat16
I32 = mybir.dt.int32
U8 = mybir.dt.uint8
U16 = mybir.dt.uint16
ALU = mybir.AluOpType
ACT = mybir.ActivationFunctionType
AX = mybir.AxisListType

P = 128
T, H, F = 2048, 256, 2048
NH = 16
HD = H // NH
EPS = 1e-5
TT = T // P
BT = 512
NB = T // BT
SUB = BT // P
PL = 2
NQ = F // P
GT = 4
NG = NQ // GT
BLK = 16
GELU_C, GELU_A = 0.7978845608028654, 0.044715
PASSES = ((0, 0), (0, 1), (1, 0))
MASKED = -1e30
CREDIT = 2
START = -3e38

NPAIR = NH // 2
HALF = 64
NPART = 3
Q_PARTS = (0, 0, 0, 1, 1, 2)
K_PARTS = (0, 1, 2, 0, 1, 0)
NKB = T // P
KR = len(Q_PARTS) * HD
SB = 3
SBANKS = 3
PRING = 8
VW = 34


def build_program(nc, h, Wq, bq, Wk, bk, Wv, bv, Wo, bo, gW, gS, uW, uS, dW, dS, out):
    nc.disable_value_cache = True
    outer = ExitStack()

    def tensors(stack, phase):
        return lambda name, shape, dt: stack.enter_context(nc.sbuf_tensor(f"{phase}_{name}", shape, dt))

    with outer:
        sb = tensors(outer, "all")
        x = sb("x", [P, TT, H], F32)
        heads = sb("heads", [P, TT, H], F32)
        w_hi = sb("w_hi", [P, 3 * NG, PL, GT * P], F32R)
        w_lo = sb("w_lo", [P, 3 * NG, PL, GT * P], F32R)
        w_part = (w_hi, w_lo)
        ident = sb("ident", [P, P], F32)
        stats = sb("stats", [P, TT, 6], F32)
        mean_var = sb("mean_var", [P, TT, 2], F32)
        var_eps = sb("var_eps", [P, TT], F32)
        deviation = sb("deviation", [P, TT], F32)
        rstd = sb("rstd", [P, TT], F32)
        psum = outer.enter_context(nc.psum_tensor("psum", [P, 8, BT], F32))
        qk_dram = nc.dram_tensor("qk_parts", (2 * NPART, H, T), BF16, kind="Internal").ap()
        v_dram = nc.dram_tensor("v_rows", (NPAIR, P, NKB, 2 * HD), F32, kind="Internal").ap()

        def as_f32(ap):
            return ap.bitcast(F32)

        def norm_stats(b):
            for i in range(SUB):
                t = b * SUB + i
                last = nc.vector.bn_stats(stats[:, bass.ds(t, 1), :].rearrange("p o c -> p (o c)"),
                                          x[:, bass.ds(t, 1), :].rearrange("p o c -> p (o c)"))
            return last

        def norm_vector(dve, s):
            for t in range(TT):
                last = nc.vector.bn_aggr(mean_var[:, t, :], stats[:, t, :])
            last.then_inc(s["aggr"], 1)
            dve.wait_ge(s["aggr"], 1)
            nc.vector.tensor_scalar(var_eps[:, :], mean_var[:, :, 1], EPS, None, ALU.add).then_inc(s["var"], 1)
            dve.wait_ge(s["std"], 1)
            nc.vector.reciprocal(rstd[:, :], deviation[:, :]).then_inc(s["rstd"], 1)
            dve.wait_ge(s["rstd"], 1)

        def norm_block(dve, s, b, use, xb):
            dve.wait_ge(s["turned"], use + 1)
            for i in range(SUB):
                t = b * SUB + i
                last = nc.vector.tensor_scalar(xb[:, i, :], x[:, bass.ds(t, 1), :].rearrange("p o c -> p (o c)"),
                                               mean_var[:, bass.ds(t, 1), 0], rstd[:, bass.ds(t, 1)],
                                               ALU.subtract, ALU.mult)
            last.then_inc(s["xb"], 1)

        def norm_scalar(act, s):
            act.wait_ge(s["var"], 1)
            nc.scalar.activation(deviation[:, :], var_eps[:, :], ACT.Sqrt).then_inc(s["std"], 1)

        def turn_tensor(xb, bank):
            for pl in range(PL):
                for i in range(SUB):
                    last = nc.tensor.transpose(psum[:, bank + pl, i * P:(i + 1) * P],
                                               xb[:, i, pl::PL], ident[:, :])
            return last

        def dequantise(s):
            with ExitStack() as st:
                tb = tensors(st, "dequant")
                codes = tb("codes", [P, 3 * NG, GT, P], I32)
                scales = tb("scales", [P, 2, NG, GT, P // BLK], F32)
                d_scales = tb("d_scales", [P, 2, F // 32], F32)
                identb = tb("identb", [P, P], BF16)
                byte = tb("byte", [P, 2, GT * P], BF16)
                wide = tb("wide", [P, 2, GT, P], F32)
                turned = tb("turned", [P, 2, GT * P], U16)
                mag = tb("mag", [P, 2, PL, GT * P], U16)
                sign = tb("sign", [P, 2, PL, GT * P], U16)
                low = tb("low", [P, 2, PL, GT * P], BF16)
                weight = tb("weight", [P, 2, PL, GT * P], F32)
                NGR = 3 * NG

                def rows(w):
                    return w.rearrange("(c p two) j -> p c two j", p=P, two=2)

                with nc.Block() as block:
                    @block.sync
                    def _(sp):
                        for m, sc in ((0, gS), (1, uS)):
                            sp.dma_start(scales[:, m, :, :, :].rearrange("p g (c two) b -> p (g c) two b", two=2),
                                         rows(sc)).then_inc(s["scales"], 16)
                        sp.dma_start(d_scales[:, :, :], dS.rearrange("(hh p) b -> p hh b", p=P)).then_inc(s["scales"], 16)
                        for g in range(NG):
                            for m, w in ((0, gW), (1, uW)):
                                sp.dma_start(codes[:, 3 * g + m, :, :].rearrange("p (c two) j -> p c two j", two=2),
                                             rows(w)[:, 2 * g:2 * g + 2]).then_inc(s[f"codes{3 * g + m}"], 16)
                            for c in range(2):
                                sp.dma_start(codes[:, 3 * g + 2, 2 * c:2 * c + 2, :],
                                             dW[:, (2 * g + c) * P:(2 * g + c + 1) * P].rearrange("(hh p) j -> p hh j", p=P)
                                             ).then_inc(s[f"codes{3 * g + 2}"], 16)
                        for t in range(0, TT, 4):
                            sp.dma_start(x[:, t:t + 4, :], h[0, t * P:(t + 4) * P, :].rearrange("(t p) c -> p t c", p=P)
                                         ).then_inc(s["x"], 16)
                        sp.wait_ge(s["x"], 16 * (TT // 4))

                    @block.gpsimd
                    def _(pool):
                        nc.gpsimd.memset(ident[:, :], 0.0).then_inc(s["ident"], 1)
                        pool.wait_ge(s["ident"], 1)
                        nc.gpsimd.affine_select(out=ident[:, :], in_=ident[:, :], compare_op=ALU.not_equal, fill=1.0,
                                                base=0, pattern=[[-1, P]], channel_multiplier=1).then_inc(s["ident"], 1)
                        pool.wait_ge(s["ident"], 2)
                        nc.gpsimd.tensor_copy(identb[:, :], ident[:, :]).then_inc(s["ident"], 1)
                        pool.wait_ge(s["scales"], 48)
                        for n in range(NGR):
                            g, m = divmod(n, 3)
                            if n >= 2:
                                pool.wait_ge(s["turned_s"], n - 1)
                            for i in range(GT):
                                src = (scales[:, m, g, i, :] if m < 2 else
                                       d_scales[:, i % 2, 8 * (2 * g + i // 2):8 * (2 * g + i // 2) + 8])
                                last = nc.gpsimd.tensor_copy(wide[:, n % 2, i, :].rearrange("p (a b) -> p a b", b=BLK),
                                                             src.unsqueeze(2).broadcast_to([P, P // BLK, BLK]))
                            last.then_inc(s["wide"], 1)

                    @block.scalar
                    def _(act):
                        for n in range(NGR + 1):
                            if n < NGR:
                                act.wait_ge(s[f"codes{n}"], 16 if n % 3 < 2 else 32)
                                if n >= 2:
                                    act.wait_ge(s["turned_c"], n - 1)
                                nc.scalar.activation(byte[:, n % 2, :],
                                                     codes[:, n, :, :].rearrange("p a b -> p (a b)").bitcast(U8)[:, ::4],
                                                     ACT.Copy).then_inc(s["byte"], 1)
                                act.wait_ge(s["turned_c"], n + 1)
                                if n >= 2:
                                    act.wait_ge(s["weight"], n - 1)
                                nc.scalar.activation(turned[:, n % 2, :], psum[:, n % 2, 0:BT // 2].bitcast(BF16),
                                                     ACT.Copy).then_inc(s["turned"], 1)
                            if n >= 1:
                                act.wait_ge(s["weight"], n)
                                nc.scalar.activation(w_hi[:, n - 1, :, :], weight[:, (n - 1) % 2, :, :],
                                                     ACT.Copy).then_inc(s["w_hi"], 1)

                    @block.tensor
                    def _(pe):
                        pe.wait_ge(s["ident"], 3)
                        for n in range(NGR):
                            pe.wait_ge(s["byte"], n + 1)
                            if n >= 2:
                                pe.wait_ge(s["turned"], n - 1)
                            for i in range(GT):
                                last = nc.tensor.transpose(psum[:, n % 2, i * HALF:(i + 1) * HALF].bitcast(BF16),
                                                           byte[:, n % 2, i * P:(i + 1) * P], identb[:, :])
                            last.then_inc(s["turned_c"], 1)
                            pe.wait_ge(s["wide"], n + 1)
                            if n >= 2:
                                pe.wait_ge(s["weight"], n - 1)
                            for i in range(GT):
                                last = nc.tensor.transpose(psum[:, 2 + n % 2, i * P:(i + 1) * P], wide[:, n % 2, i, :],
                                                           ident[:, :])
                            last.then_inc(s["turned_s"], 1)

                    @block.vector
                    def _(dve):
                        def own(instruction, count):
                            instruction.then_inc(s["step"], 1)
                            dve.wait_ge(s["step"], count)

                        for n in range(NGR):
                            code, m, sg, lw = turned[:, n % 2, :], mag[:, n % 2], sign[:, n % 2], low[:, n % 2]
                            dve.wait_ge(s["turned"], n + 1)
                            nc.vector.tensor_scalar(m[:, 0, :], code, 0xF8, 6, ALU.bitwise_or, ALU.logical_shift_left)
                            nc.vector.tensor_scalar(sg[:, 0, :], code, 0x08, 12, ALU.bitwise_and, ALU.logical_shift_left)
                            nc.vector.tensor_scalar(sg[:, 1, :], code, 0x80, 8, ALU.bitwise_and, ALU.logical_shift_left)
                            own(nc.vector.tensor_scalar(m[:, 1, :], code, 0x70, 0xF80, ALU.bitwise_and, ALU.bitwise_or), 4 * n + 1)
                            own(nc.vector.tensor_scalar(m[:, 1, :], m[:, 1, :], 2, None, ALU.logical_shift_left), 4 * n + 2)
                            g8 = m.bitcast(BF16)
                            own(nc.vector.tensor_scalar(lw, g8, 8.0, -1.0, ALU.mult, ALU.add), 4 * n + 3)
                            nc.vector.scalar_tensor_tensor(g8, g8, 4.0, lw, ALU.mult, ALU.min).then_inc(s["value"], 1)
                            dve.wait_ge(s["value"], 2 * n + 1)
                            nc.vector.tensor_tensor(m, m, sg, ALU.bitwise_or).then_inc(s["value"], 1)
                            dve.wait_ge(s["value"], 2 * n + 2)
                            dve.wait_ge(s["turned_s"], n + 1)
                            if n >= 2:
                                dve.wait_ge(s["w_hi"], n - 1)
                            nc.vector.tensor_tensor(weight[:, n % 2], g8,
                                                    psum[:, 2 + n % 2, :].unsqueeze(1).broadcast_to([P, PL, BT]),
                                                    ALU.mult).then_inc(s["weight"], 1)
                            dve.wait_ge(s["w_hi"], n + 1)
                            own(nc.vector.tensor_tensor(w_lo[:, n], weight[:, n % 2], as_f32(w_hi[:, n]), ALU.subtract), 4 * n + 4)
                        dve.wait_ge(s["x"], 16 * NB)
                        for b in range(NB):
                            norm_stats(b)

        def ffn(phase, s, store):
            with ExitStack() as st:
                tb = tensors(st, phase)
                xb = tb("xb", [P, SUB, H], F32)
                xt = tb("xt", [P, 2, 2, PL, BT], F32R)
                inner = tb("inner", [P, 2, 2, BT], F32R)
                arg = tb("arg", [P, 2, BT], F32)
                act_out = tb("act_out", [P, 2, BT], F32)
                ACC = 6
                SPLIT = NQ // 2

                def loop(engine, block_steps):
                    with engine.Fori(0, NB // 2) as it:
                        block_steps(it * 2, 0, it * 2 + 1)
                        block_steps(it * 2 + 1, 1, it * -2 + 2)

                with nc.Block() as block:
                    @block.tensor
                    def _(pe):
                        def turn(use):
                            pe.wait_ge(s["xb"], use + 1)
                            if not isinstance(use, int):
                                pe.wait_ge(s["xt_lo"], use)
                            turn_tensor(xb, 4).then_inc(s["turned"], 1)

                        def gate_up(b, k, q):
                            pe.wait_ge(s["product"], b * NQ + q + 1)
                            g, o = q // GT, (q % GT) * P
                            for m in range(2):
                                n = 0
                                for pl in range(PL):
                                    for a, c in PASSES:
                                        last = nc.tensor.matmul(psum[:, 2 * m + q % 2, :],
                                                                w_part[a][:, 3 * g + m, pl, o:o + P], xt[:, k, c, pl, :],
                                                                start=(n == 0), stop=(n == 5))
                                        n += 1
                            last.then_inc(s["gu"], 1)

                        def down(b, q):
                            pe.wait_ge(s["inner_lo"], b * NQ + q + 1 + CREDIT)
                            if q == 0:
                                pe.wait_ge(s["added"], b + 1)
                            c, pl = divmod(q, 2)
                            for i in range(SUB):
                                for n, (a, e) in enumerate(PASSES):
                                    last = nc.tensor.matmul(psum[:, ACC + i // 2, (i % 2) * H:(i % 2 + 1) * H],
                                                            inner[:, a, q % 2, i * P:(i + 1) * P],
                                                            w_part[e][:, 3 * (c // 2) + 2, pl, (c % 2) * H:(c % 2 + 1) * H],
                                                            start=(q == 0 and n == 0 and i % 2 == 0),
                                                            stop=(q == NQ - 1 and n == 2), skip_group_check=True)
                            last.then_inc(s["down"], 1)

                        def block_steps(b, k, following):
                            pe.wait_ge(s["xt_lo"], b + 1)
                            for q in range(NQ):
                                gate_up(b, k, q)
                                if q == SPLIT:
                                    turn(b + 1)
                                if q >= 2:
                                    down(b, q - 2)
                                elif k == 1:
                                    down(b - 1, NQ - 2 + q)
                            if k == 1:
                                down(b, NQ - 2)
                                down(b, NQ - 1)

                        turn(0)
                        loop(nc.tensor, block_steps)

                    @block.scalar
                    def _(act):
                        norm_scalar(act, s)

                        def split(use, k):
                            act.wait_ge(s["turned"], use + 2)
                            nc.scalar.activation(xt[:, k, 0, :, :], psum[:, 4:6, :], ACT.Copy).then_inc(s["xt_hi"], 1)

                        def high_part(b, q):
                            u = q % 2
                            n = b * NQ + q
                            act.wait_ge(s["product"], n + 1 + CREDIT)
                            act.wait_ge(s["down"], n + 1)
                            nc.scalar.activation(inner[:, 0, u, :], act_out[:, u, :], ACT.Copy).then_inc(s["inner_hi"], 1)

                        def block_steps(b, k, following):
                            for q in range(NQ):
                                n = b * NQ + q
                                u = q % 2
                                act.wait_ge(s["gu"], n + 1)
                                act.wait_ge(s["tanh"], n + 1)
                                nc.scalar.activation(arg[:, u, :], psum[:, u, :], ACT.Square).then_inc(s["square"], 1)
                                if q >= 1:
                                    high_part(b, q - 1)
                                elif k == 1:
                                    high_part(b - 1, NQ - 1)
                                act.wait_ge(s["cubic"], n + 1)
                                act.wait_ge(s["inner_lo"], n + 1)
                                nc.scalar.activation(act_out[:, u, :], arg[:, u, :], ACT.Tanh,
                                                     scale=GELU_C).then_inc(s["tanh"], 1)
                                if q == SPLIT + 1:
                                    split(b + 1, 1 - k)
                            if k == 1:
                                high_part(b, NQ - 1)

                        act.sem_inc(s["tanh"], CREDIT)
                        split(0, 0)
                        loop(nc.scalar, block_steps)

                    @block.vector
                    def _(dve):
                        dve.sem_inc(s["product"], CREDIT)
                        dve.sem_inc(s["inner_lo"], CREDIT)
                        dve.sem_inc(s["added"], 1)
                        norm_vector(dve, s)

                        def split(use, k):
                            dve.wait_ge(s["xt_hi"], use + 1)
                            nc.vector.tensor_tensor(xt[:, k, 1, :, :], psum[:, 4:6, :], as_f32(xt[:, k, 0, :, :]),
                                                    ALU.subtract).then_inc(s["xt_lo"], 1)

                        def low_part(b, q):
                            u = q % 2
                            dve.wait_ge(s["inner_hi"], b * NQ + q + 1)
                            nc.vector.tensor_tensor(inner[:, 1, u, :], act_out[:, u, :], as_f32(inner[:, 0, u, :]),
                                                    ALU.subtract).then_inc(s["inner_lo"], 1)

                        def add(b):
                            dve.wait_ge(s["down"], (b + 1) * NQ + CREDIT)
                            for j in range(2):
                                dst = x[:, bass.ds(b * SUB + 2 * j, 2), :].rearrange("p a c -> p (a c)")
                                last = nc.vector.scalar_tensor_tensor(dst, psum[:, ACC + j, :], 0.5, dst, ALU.mult, ALU.add)
                            last.then_inc(s["added"], 1)
                            if not store:
                                dve.wait_ge(s["added"], b + 2)
                                norm_stats(b)

                        def block_steps(b, k, following):
                            for q in range(NQ):
                                n = b * NQ + q
                                u = q % 2
                                dve.wait_ge(s["square"], n + 1)
                                nc.vector.tensor_scalar(arg[:, u, :], arg[:, u, :], GELU_A, 1.0, ALU.mult,
                                                        ALU.add).then_inc(s["quadratic"], 1)
                                dve.wait_ge(s["quadratic"], n + 1)
                                nc.vector.tensor_tensor(arg[:, u, :], arg[:, u, :], psum[:, u, :],
                                                        ALU.mult).then_inc(s["cubic"], 1)
                                if q >= 1:
                                    low_part(b, q - 1)
                                elif k == 1:
                                    low_part(b - 1, NQ - 1)
                                if q == 2 and k == 1:
                                    add(b - 1)
                                if q == SPLIT - 2:
                                    norm_block(dve, s, following, b + 1, xb)
                                if q == SPLIT + 2:
                                    split(b + 1, 1 - k)
                                dve.wait_ge(s["tanh"], n + 1 + CREDIT)
                                nc.vector.scalar_tensor_tensor(act_out[:, u, :], act_out[:, u, :], 1.0, psum[:, u, :],
                                                               ALU.add, ALU.mult).then_inc(s["gelu"], 1)
                                dve.wait_ge(s["gelu"], n + 1)
                                nc.vector.scalar_tensor_tensor(act_out[:, u, :], act_out[:, u, :], 0.5, psum[:, 2 + u, :],
                                                               ALU.mult, ALU.mult).then_inc(s["product"], 1)
                            if k == 1:
                                low_part(b, NQ - 1)
                                add(b)

                        norm_block(dve, s, 0, 0, xb)
                        split(0, 0)
                        loop(nc.vector, block_steps)

                    @block.gpsimd
                    def _(pool):
                        pool.sem_inc(s["down"], CREDIT)
                        pool.sem_inc(s["turned"], 1)

                    @block.sync
                    def _(sp):
                        if store:
                            with nc.sync.Fori(0, NB) as b:
                                sp.wait_ge(s["added"], b + 2)
                                sp.dma_start(out[0, bass.ds(b * BT, BT), :].rearrange("(t p) c -> p t c", p=P),
                                             x[:, bass.ds(b * SUB, SUB), :]).then_inc(s["stored"], 16)
                            sp.wait_ge(s["stored"], 16 * NB)

        def qkv(s):
            with ExitStack() as st:
                tb = tensors(st, "qkv")
                raw = tb("raw", [P, 3, 2, H], F32)
                wt = tb("wt", [P, 2, 3, PL, H], F32R)
                wfull = tb("wfull", [P, 3, PL, H], F32)
                bias = tb("bias", [P, 2, 2], F32)
                bias_v = tb("bias_v", [P, H], F32)
                xb = tb("xb", [P, SUB, H], F32)
                xt = tb("xt", [P, 2, 2, PL, BT], F32R)
                NU = 4
                full = tb("full", [P, NU, BT], F32)
                rest = tb("rest", [P, NU, BT], F32)
                parts = tb("parts", [P, NU, NPART, BT], BF16)
                rows_v = tb("rows_v", [P, SUB, H], F32)
                bias_q = tb("bias_q", [P, 2], F32)
                SCALE = HD ** -0.5

                def loop(engine, block_steps):
                    with engine.Fori(0, NB // 2) as it:
                        block_steps(it * 2, 0, it * 2 + 1)
                        block_steps(it * 2 + 1, 1, it * -2 + 2)

                with nc.Block() as block:
                    @block.sync
                    def _(sp):
                        for m, w in enumerate((Wq, Wk, Wv)):
                            sp.dma_start(raw[:, m, :, :], w.rearrange("(hh p) c -> p hh c", p=P)).then_inc(s["loaded"], 16)
                        for m, b_ in enumerate((bq, bk)):
                            sp.dma_start(bias[:, m, :], b_.rearrange("(hh p) -> p hh", p=P),
                                         allow_slow_non_contiguous=True).then_inc(s["loaded"], 16)
                        sp.dma_start(bias_v[:, :], bv.rearrange("(o c) -> o c", o=1).broadcast_to([P, H])).then_inc(s["loaded"], 16)

                        def block_steps(b, k, following):
                            for u in range(NU):
                                kind, half = divmod(u, 2)
                                sp.wait_ge(s["part_3"], b * NU + u + 1)
                                sp.dma_start(qk_dram[NPART * kind:NPART * (kind + 1), half * P:(half + 1) * P, bass.ds(b * BT, BT)]
                                             .rearrange("a p t -> p a t"), parts[:, u, :, :]).then_inc(s[f"part_out{u}"], 16)
                            sp.wait_ge(s["v"], (b + 1) * SUB + CREDIT)
                            for i in range(SUB):
                                sp.dma_start(v_dram[:, :, bass.ds(b * SUB + i, 1), :].rearrange("r p o c -> p r (o c)"),
                                             rows_v[:, i, :].rearrange("p (r c) -> p r c", c=2 * HD)).then_inc(s[f"v_out{i}"], 16)

                        loop(nc.sync, block_steps)
                        for u in range(NU):
                            sp.wait_ge(s[f"part_out{u}"], 16 + 16 * NB)
                            sp.wait_ge(s[f"v_out{u}"], 16 + 16 * NB)

                    @block.tensor
                    def _(pe):
                        def turn(use):
                            pe.wait_ge(s["xb"], use + 1)
                            if not isinstance(use, int):
                                pe.wait_ge(s["xt_lo"], use)
                            turn_tensor(xb, 4).then_inc(s["turned"], 1)

                        def block_steps(b, k, following):
                            pe.wait_ge(s["xt_lo"], b + 1)
                            for u in range(NU):
                                kind, half = divmod(u, 2)
                                pe.wait_ge(s["full"], b * NU + u + 1)
                                n = 0
                                for pl in range(PL):
                                    for a, c in PASSES:
                                        last = nc.tensor.matmul(psum[:, u, :], wt[:, a, kind, pl, half * P:(half + 1) * P],
                                                                xt[:, k, c, pl, :], start=(n == 0), stop=(n == 5))
                                        n += 1
                                last.then_inc(s["unit"], 1)
                                if u == 0:
                                    turn(b + 1)
                            for i in range(SUB):
                                pe.wait_ge(s["v"], b * SUB + i + 1)
                                n = 0
                                for pl in range(PL):
                                    for a, c in PASSES:
                                        last = nc.tensor.matmul(psum[:, 6 + i % 2, 0:H], xt[:, k, a, pl, i * P:(i + 1) * P],
                                                                wt[:, c, 2, pl, :], start=(n == 0), stop=(n == 5))
                                        n += 1
                                last.then_inc(s["v_sum"], 1)

                        pe.wait_ge(s["loaded"], 96)
                        for m in range(3):
                            if m == 2:
                                pe.wait_ge(s["wfull"], 1)
                            for pl in range(PL):
                                for hh in range(2):
                                    last = nc.tensor.transpose(psum[:, 2 * (m % 2) + pl, hh * P:(hh + 1) * P],
                                                               raw[:, m, hh, pl::PL], ident[:, :])
                            last.then_inc(s["wt"], 1)
                        turn(0)
                        pe.wait_ge(s["wt_lo"], 3)
                        loop(nc.tensor, block_steps)

                    @block.scalar
                    def _(act):
                        def split(use, k):
                            act.wait_ge(s["turned"], use + 2)
                            nc.scalar.activation(xt[:, k, 0, :, :], psum[:, 4:6, :], ACT.Copy).then_inc(s["xt_hi"], 1)

                        def part(b, u, j):
                            n = b * NU + u
                            if j == 0:
                                act.wait_ge(s["full"], n + 1 + NU)
                                act.wait_ge(s[f"part_out{u}"], (b + 1) * 16)
                            else:
                                act.wait_ge(s["rest"], n + 1)
                            nc.scalar.activation(parts[:, u, j, :], (full if j == 0 else rest)[:, u, :],
                                                 ACT.Copy).then_inc(s[f"part_{j + 1}"], 1)

                        def block_steps(b, k, following):
                            for u in range(NU):
                                kind, half = divmod(u, 2)
                                act.wait_ge(s["unit"], b * NU + u + 1)
                                nc.scalar.activation(full[:, u, :], psum[:, u, :], ACT.Identity,
                                                     scale=SCALE if kind == 0 else 1.0,
                                                     bias=bias_q[:, half:half + 1] if kind == 0 else bias[:, 1, half:half + 1]
                                                     ).then_inc(s["full"], 1)
                                part(b, u, 0)
                                if u == 1:
                                    split(b + 1, 1 - k)
                                if u:
                                    part(b, u - 1, 1)
                            part(b, NU - 1, 1)
                            act.wait_ge(s["part_3"], (b + 1) * NU)

                        norm_scalar(act, s)
                        act.wait_ge(s["loaded"], 96)
                        nc.scalar.activation(bias_q[:, :], bias[:, 0, :], ACT.Copy, scale=SCALE).then_inc(s["bias_q"], 1)
                        for m in range(3):
                            act.wait_ge(s["wt"], m + 1)
                            nc.scalar.activation(wfull[:, m, :, :], psum[:, 2 * (m % 2):2 * (m % 2) + 2, 0:H], ACT.Copy).then_inc(s["wfull"], 1)
                        split(0, 0)
                        act.wait_ge(s["bias_q"], 1)
                        act.sem_inc(s["full"], NU)
                        loop(nc.scalar, block_steps)

                    @block.vector
                    def _(dve):
                        def split(use, k):
                            dve.wait_ge(s["xt_hi"], use + 1)
                            nc.vector.tensor_tensor(xt[:, k, 1, :, :], psum[:, 4:6, :], as_f32(xt[:, k, 0, :, :]),
                                                    ALU.subtract).then_inc(s["xt_lo"], 1)

                        def lesser(b, u, j):
                            n = b * NU + u
                            dve.wait_ge(s[f"part_{j + 1}"], n + 1)
                            if j == 0:
                                nc.vector.tensor_tensor(rest[:, u, :], full[:, u, :], parts[:, u, 0, :], ALU.subtract).then_inc(s["rest"], 1)
                            else:
                                nc.vector.tensor_tensor(parts[:, u, 2, :], rest[:, u, :], parts[:, u, 1, :], ALU.subtract).then_inc(s["part_3"], 1)

                        def block_steps(b, k, following):
                            norm_block(dve, s, following, b + 1, xb)
                            for u in range(NU):
                                lesser(b, u, 0)
                                if u == 1:
                                    split(b + 1, 1 - k)
                                if u:
                                    lesser(b, u - 1, 1)
                            lesser(b, NU - 1, 1)
                            for i in range(SUB):
                                dve.wait_ge(s["v_sum"], b * SUB + i + 1)
                                dve.wait_ge(s[f"v_out{i}"], (b + 1) * 16)
                                nc.vector.tensor_tensor(rows_v[:, i, :], psum[:, 6 + i % 2, 0:H], bias_v[:, :],
                                                        ALU.add).then_inc(s["v"], 1)

                        dve.sem_inc(s["v"], CREDIT)
                        norm_vector(dve, s)
                        norm_block(dve, s, 0, 0, xb)
                        for m in range(3):
                            dve.wait_ge(s["wfull"], m + 1)
                            nc.vector.tensor_copy(wt[:, 0, m, :, :], wfull[:, m, :, :]).then_inc(s["wt_hi"], 1)
                            dve.wait_ge(s["wt_hi"], m + 1)
                            nc.vector.tensor_tensor(wt[:, 1, m, :, :], wfull[:, m, :, :], as_f32(wt[:, 0, m, :, :]),
                                                    ALU.subtract).then_inc(s["wt_lo"], 1)
                        split(0, 0)
                        loop(nc.vector, block_steps)

                    @block.gpsimd
                    def _(pool):
                        pool.sem_inc(s["turned"], 1)
                        for u in range(NU):
                            pool.sem_inc(s[f"part_out{u}"], 16)
                            pool.sem_inc(s[f"v_out{u}"], 16)

        def attention(s):
            steps = [(qt, kb) for qt in range(NB) for kb in range(0, SUB * (qt + 1), 2)]
            NS = len(steps)
            NT = 4 * NS
            chunks = [(i, c) for i in range(TT) for c in range(i // SUB + 1)]
            NM = 2 * len(chunks)
            LEAD = NS - 3
            quota = [len(chunks) * min(d + 1, LEAD) // LEAD for d in range(NS)]
            S0, M0, O0, X0 = 0, 3, 5, 7

            def first_query(qt, kb):
                at = max(0, P * (kb - SUB * qt))
                return 0 if (qt, kb) == (0, 1) else at

            masks = [(d, 2 * k + hd) for d, (qt, kb) in enumerate(steps) if kb >= SUB * qt for k in range(2) for hd in range(2)]
            NMASK = len(masks)

            with ExitStack() as st:
                tb = tensors(st, "attn")
                stack = tb("stack", [P, SB, 2, 2, T], BF16)
                prob = tb("prob", [P, PRING, BT], F32)
                vals = tb("vals", [P, SB, NKB, VW], F32)
                o_sb = tb("o_sb", [P, 2, BT], F32)
                pick = tb("pick", [P, VW], F32)
                mask = tb("mask", [P, BT], BF16)
                junk = tb("junk", [P, BT], BF16)
                part_max = tb("part_max", [P, 2, TT, NB], F32)
                row_max = tb("row_max", [P, 2, TT], F32)
                max_rest = tb("max_rest", [P, 2, TT], F32)
                max_parts = tb("max_parts", [P, 2, NPART, TT], BF16)
                max_rows = tb("max_rows", [2 * NPART * TT, P], BF16)
                identb = tb("identb", [P, P], BF16)
                rden = tb("rden", [P, SUB, 2], F32)

                def alone(engine, s):
                    engine.sem_inc(s["passed"], 1)

                def q_of(b, hd):
                    return stack[:, b, hd, 0, :]

                def k_of(b, hd):
                    return stack[:, b, hd, 1, :]

                def loop(engine, body):
                    with engine.Fori(0, NPAIR // SB) as it:
                        for r in range(SB):
                            body(it * SB + r, it, r, True)
                    for r in range(NPAIR % SB):
                        it = NPAIR // SB
                        body(it * SB + r, it, r, r < NPAIR % SB - 1)

                def loaded(it, r):
                    return (it + r // SB + 1) * 19 * 16

                with nc.Block() as block:
                    @block.sync
                    def _(sp):
                        def load(p, b):
                            for hd in range(2):
                                rows = bass.ds(p * 2 * HD + hd * HD, HD)
                                q, k = q_of(b, hd), k_of(b, hd)
                                for j, part in enumerate(Q_PARTS):
                                    sp.dma_start(q[j * HD:(j + 1) * HD, :], qk_dram[part, rows, :]).then_inc(s[f"stack{b}"], 16)
                                for j, n in ((0, 3), (3, 2), (5, 1)):
                                    sp.dma_start(k[j * HD:(j + n) * HD, :], qk_dram[NPART:NPART + n, rows, :]).then_inc(s[f"stack{b}"], 16)
                            sp.dma_start(vals[:, b, :, 1:1 + 2 * HD], v_dram[bass.ds(p, 1), :, :, :].rearrange("o p k c -> p (o k) c")
                                         ).then_inc(s[f"stack{b}"], 16)

                        def max_row(p, b):
                            sp.wait_ge(s["max_rows"], p + 1)
                            for hd in range(2):
                                sp.dma_start(q_of(b, hd)[KR:KR + NPART, :], max_rows[NPART * hd * TT:NPART * (hd + 1) * TT, :]
                                             ).then_inc(s["max_loaded"], 16)

                        sp.wait_ge(s["ones"], 2 * SB + 3)
                        load(0, 0)
                        load(1, 1)
                        max_row(0, 0)

                        def pair(p, it, r, more):
                            if not isinstance(p, int):
                                sp.wait_ge(s["scored"], p * NT + 1)
                                sp.wait_ge(s["weighted"], p * NS + CREDIT)
                                load(p + 2, (r + 2) % SB)
                            if more:
                                max_row(p + 1, (r + 1) % SB)

                        loop(nc.sync, pair)

                    @block.gpsimd
                    def _(pool):
                        for b in range(SB):
                            for hd in range(2):
                                nc.gpsimd.memset(k_of(b, hd)[KR:P, :], -1.0).then_inc(s["ones"], 1)
                        pool.wait_ge(s["ones"], 2 * SB)
                        nc.gpsimd.memset(vals[:, :, :, 0:1], 1.0).then_inc(s["ones"], 1)
                        nc.gpsimd.memset(vals[:, :, :, VW - 1:VW], 1.0).then_inc(s["ones"], 1)
                        nc.gpsimd.memset(part_max[:, :, :, :], START).then_inc(s["mask"], 1)
                        nc.gpsimd.tensor_copy(identb[:, :], ident[:, :]).then_inc(s["ones"], 1)
                        nc.gpsimd.memset(mask[:, :], 0.0).then_inc(s["mask"], 1)
                        nc.gpsimd.memset(pick[:, :], 0.0).then_inc(s["mask"], 1)
                        pool.wait_ge(s["mask"], 3)
                        nc.gpsimd.affine_select(out=mask[:, BT - P:BT], in_=mask[:, BT - P:BT], compare_op=ALU.is_ge, fill=MASKED,
                                                base=0, pattern=[[-1, P]], channel_multiplier=1).then_inc(s["mask"], 1)
                        n = 4
                        for hd, (first, den) in enumerate(((1, 0), (HD - 1, 2 * HD - 1))):
                            for k in range(2):
                                row = 32 * (2 * hd + k)
                                for cols, r in ((pick[:, hd * HD:(hd + 1) * HD], row + first), (pick[:, 2 * HD + hd:2 * HD + hd + 1], row + den)):
                                    pool.wait_ge(s["mask"], n)
                                    nc.gpsimd.affine_select(out=cols, in_=cols, compare_op=ALU.not_equal, fill=1.0, base=-r,
                                                            pattern=[[-1, cols.shape[1]]], channel_multiplier=1).then_inc(s["mask"], 1)
                                    n += 1

                        def pair(p, it, r, more):
                            for n, (d, j) in enumerate(masks):
                                qt, kb = steps[d]
                                kb += j // 2
                                at = first_query(qt, kb)
                                wide = 2 * P if (qt, kb) == (0, 1) else P
                                t = prob[:, (4 * d + j) % PRING, at:at + wide]
                                pool.wait_ge(s["exp"], p * NT + 4 * d + j + 1 + SBANKS)
                                alone(pool, s)
                                nc.gpsimd.affine_select(out=t, in_=t, compare_op=ALU.is_ge, fill=0.0, base=P - wide,
                                                        pattern=[[1, wide]], channel_multiplier=-1).then_inc(s["masked"], 1)

                        loop(nc.gpsimd, pair)

                    @block.tensor
                    def _(pe):
                        pe.wait_ge(s["mask"], 12)
                        pe.wait_ge(s["ones"], 2 * SB + 3)

                        def score(p, b, d, j):
                            k, hd = divmod(j, 2)
                            qt, kb = steps[d]
                            at = first_query(qt, kb + k)
                            n = 4 * d + j
                            rows = slice(0, KR + NPART)
                            pe.wait_ge(s["exp"], p * NT + n + 1)
                            nc.tensor.matmul(psum[:, S0 + (b * NT + n) % SBANKS, at:BT], k_of(b, hd)[rows, (kb + k) * P:(kb + k + 1) * P],
                                             q_of(b, hd)[rows, qt * BT + at:(qt + 1) * BT], start=True, stop=True).then_inc(s["scored"], 1)

                        def maxima(p, b, m):
                            i, c = chunks[m]
                            cols = BT if c < i // SUB else P * (i % SUB + 1)
                            for hd in range(2):
                                pe.wait_ge(s["max_read"], p * NM + 2 * m + hd + 1)
                                nc.tensor.matmul(psum[:, M0 + hd, 0:cols], q_of(b, hd)[0:KR, i * P:(i + 1) * P],
                                                 k_of(b, hd)[0:KR, c * BT:c * BT + cols], start=True, stop=True).then_inc(s["max_scored"], 1)

                        def turn_max(p):
                            pe.wait_ge(s["max_parts"], p + 1)
                            if not (isinstance(p, int) and p == 0):
                                pe.wait_ge(s["normed"], p * NB)
                            alone(pe, s)
                            nc.tensor.transpose(psum[0:2 * NPART * TT, X0, 0:HALF].bitcast(BF16),
                                                max_parts[:, :, :, :].rearrange("p a b c -> p (a b c)"), identb[:, :]).then_inc(s["max_turned"], 1)

                        def weigh(p, b, d):
                            qt, kb = steps[d]
                            pe.wait_ge(s["exp"], p * NT + 4 * d + 4 + SBANKS)
                            done = sum(1 for e, _ in masks if e <= d)
                            if kb >= SUB * qt:
                                pe.wait_ge(s["masked"], p * NMASK + done)
                            if kb == 0:
                                pe.wait_ge(s["o_copied"], p * NB + qt + 1)
                            for hd in range(2):
                                for k in range(2):
                                    at = first_query(qt, kb + k)
                                    r = 32 * (2 * hd + k)
                                    last = nc.tensor.matmul(psum[r:r + 32, O0 + qt % 2, at:BT], vals[:, b, kb + k, 2 * hd:2 * hd + 32],
                                                            prob[:, (4 * d + 2 * k + hd) % PRING, at:BT], start=(kb == 0),
                                                            stop=(kb == SUB * (qt + 1) - 2), skip_group_check=True)
                            last.then_inc(s["weighted"], 1)

                        def gather(p, qt):
                            pe.wait_ge(s["o_copied"], p * NB + qt + 1 + CREDIT)
                            pe.wait_ge(s["max_rows"], p + 1)
                            if qt == NB - 1 and not (isinstance(p, int) and p == NPAIR - 1):
                                pe.wait_ge(s["max_rows"], p + 2)
                            pe.wait_ge(s["normed"], p * NB + qt + 1)
                            for i in range(SUB):
                                last = nc.tensor.matmul(psum[:, X0, i * VW:(i + 1) * VW], o_sb[:, qt % 2, i * P:(i + 1) * P], pick[:, :],
                                                        start=True, stop=True)
                            last.then_inc(s["gathered"], 1)

                        def pair(p, it, r, more):
                            nb = (r + 1) % SB
                            pe.wait_ge(s["max_loaded"], 32 * (p + 1))
                            if more:
                                pe.wait_ge(s[f"stack{nb}"], loaded(it, r + 1))
                            for d in range(NS):
                                before = quota[d - 1] if d else 0
                                middle = (before + quota[d]) // 2
                                for k, ms in enumerate((range(before, middle), range(middle, quota[d]))):
                                    score(p, r, d, 2 * k)
                                    score(p, r, d, 2 * k + 1)
                                    if more:
                                        for m in ms:
                                            maxima(p + 1, nb, m)
                                if d >= 1:
                                    weigh(p, r, d - 1)
                                if d >= 2 and steps[d - 1][0] != steps[d - 2][0]:
                                    gather(p, steps[d - 2][0])
                                if d == NS - 2 and more:
                                    turn_max(p + 1)
                            weigh(p, r, NS - 1)
                            gather(p, NB - 1)

                        pe.wait_ge(s["stack0"], loaded(0, 0))
                        for m in range(len(chunks)):
                            maxima(0, 0, m)
                        turn_max(0)
                        loop(nc.tensor, pair)

                    @block.scalar
                    def _(act):
                        def copy_max(p):
                            act.wait_ge(s["max_turned"], p + 1)
                            act.wait_ge(s["max_loaded"], 32 * p)
                            nc.scalar.activation(max_rows[:, :], psum[0:2 * NPART * TT, X0, 0:HALF].bitcast(BF16), ACT.Copy).then_inc(s["max_rows"], 1)

                        def copy_out(p, qt):
                            act.wait_ge(s["weighted"], p * NS + sum(1 for e in steps if e[0] <= qt) + CREDIT)
                            act.wait_ge(s["gathered"], p * NB + qt + 1)
                            nc.scalar.activation(o_sb[:, qt % 2, :], psum[:, O0 + qt % 2, :], ACT.Copy).then_inc(s["o_copied"], 1)

                        def pair(p, it, r, more):
                            for d, (qt, kb) in enumerate(steps):
                                act.wait_ge(s["weighted"], p * NS + d + 1)
                                for j in range(4):
                                    at = first_query(qt, kb + j // 2)
                                    n = 4 * d + j
                                    act.wait_ge(s["scored"], p * NT + n + 1)
                                    nc.scalar.activation(prob[:, n % PRING, at:BT], psum[:, S0 + (r * NT + n) % SBANKS, at:BT],
                                                         ACT.Exp).then_inc(s["exp"], 1)
                                if d >= 1 and steps[d - 1][0] != qt:
                                    copy_out(p, qt - 1)
                                if d == NS - 2 and more:
                                    copy_max(p + 1)
                            copy_out(p, NB - 1)

                        act.sem_inc(s["exp"], SBANKS)
                        act.sem_inc(s["o_copied"], CREDIT)
                        act.wait_ge(s["max_turned"], 1)
                        nc.scalar.activation(max_rows[:, :], psum[0:2 * NPART * TT, X0, 0:HALF].bitcast(BF16), ACT.Copy).then_inc(s["max_rows"], 1)
                        loop(nc.scalar, pair)

                    @block.vector
                    def _(dve):
                        def maxima(p, m):
                            i, c = chunks[m]
                            if m == 0 and not (isinstance(p, int) and p == 0):
                                dve.wait_ge(s["row_max"], p)
                            diagonal = [e for e in range(m) if chunks[e][1] == chunks[e][0] // SUB]
                            for hd in range(2):
                                dve.wait_ge(s["max_scored"], p * NM + 2 * m + hd + 1)
                                to = part_max[:, hd, i, c:c + 1]
                                if c < i // SUB:
                                    nc.vector.tensor_reduce(to, psum[:, M0 + hd, :], AX.X, ALU.max).then_inc(s["max_read"], 1)
                                else:
                                    cols = P * (i % SUB + 1)
                                    dve.wait_ge(s["max_read"], p * NM + (2 * m + hd if hd else 2 * diagonal[-1] + 2 if diagonal else 0) + CREDIT)
                                    alone(dve, s)
                                    nc.vector.tensor_tensor_reduce(out=junk[:, 0:cols], in0=psum[:, M0 + hd, 0:cols],
                                                                   in1=mask[:, BT - cols:BT], scale=1.0, scalar=START,
                                                                   op0=ALU.add, op1=ALU.max, accum_out=to).then_inc(s["max_read"], 1)

                        def split_max(p):
                            dve.wait_ge(s["max_read"], (p + 1) * NM + CREDIT)
                            if not (isinstance(p, int) and p == 0):
                                dve.wait_ge(s["max_turned"], p)
                            nc.vector.tensor_reduce(row_max[:, :, :], part_max[:, :, :, :], AX.X, ALU.max).then_inc(s["row_max"], 1)
                            dve.wait_ge(s["row_max"], p + 1)
                            nc.vector.tensor_copy(max_parts[:, :, 0, :], row_max[:, :, :]).then_inc(s["max_step"], 1)
                            dve.wait_ge(s["max_step"], 4 * p + 1)
                            nc.vector.tensor_tensor(max_rest[:, :, :], row_max[:, :, :], max_parts[:, :, 0, :],
                                                    ALU.subtract).then_inc(s["max_step"], 1)
                            dve.wait_ge(s["max_step"], 4 * p + 2)
                            nc.vector.tensor_copy(max_parts[:, :, 1, :], max_rest[:, :, :]).then_inc(s["max_step"], 1)
                            dve.wait_ge(s["max_step"], 4 * p + 3)
                            nc.vector.tensor_tensor(max_parts[:, :, 2, :], max_rest[:, :, :], max_parts[:, :, 1, :],
                                                    ALU.subtract).then_inc(s["max_parts"], 1)
                            dve.wait_ge(s["max_parts"], p + 1)
                            dve.sem_inc(s["max_step"], 1)

                        def normalise(p, qt):
                            dve.wait_ge(s["gathered"], p * NB + qt + 1 + CREDIT)
                            got = psum[:, X0, 0:SUB * VW].rearrange("p (i c) -> p i c", c=VW)
                            dve.wait_ge(s["normed"], p * NB + qt + 1)
                            nc.vector.reciprocal(rden[:, :, :], got[:, :, 2 * HD:]).then_inc(s["rden"], 1)
                            dve.wait_ge(s["rden"], p * NB + qt + 1)
                            nc.vector.tensor_tensor(heads[:, qt * SUB:(qt + 1) * SUB, bass.ds(p * 2 * HD, 2 * HD)].rearrange(
                                                        "p i (a c) -> p i a c", c=HD),
                                                    got[:, :, 0:2 * HD].rearrange("p i (a c) -> p i a c", c=HD),
                                                    rden[:, :, :].unsqueeze(3).broadcast_to([P, SUB, 2, HD]),
                                                    ALU.mult).then_inc(s["normed"], 1)

                        def pair(p, it, r, more):
                            for d in range(NS):
                                if more:
                                    for m in range(quota[d - 1] if d else 0, quota[d]):
                                        maxima(p + 1, m)
                                    if quota[d] == len(chunks) and (d == 0 or quota[d - 1] < len(chunks)):
                                        split_max(p + 1)
                                if d >= 2 and steps[d - 1][0] != steps[d - 2][0]:
                                    normalise(p, steps[d - 2][0])
                            normalise(p, NB - 1)

                        dve.sem_inc(s["max_read"], CREDIT)
                        dve.sem_inc(s["gathered"], CREDIT)
                        dve.sem_inc(s["normed"], 1)
                        dve.sem_inc(s["weighted"], CREDIT)
                        dve.wait_ge(s["mask"], 12)
                        for m in range(len(chunks)):
                            maxima(0, m)
                        split_max(0)
                        loop(nc.vector, pair)

        def project(s):
            with ExitStack() as st:
                tb = tensors(st, "proj")
                raw = tb("raw_o", [P, 2, H], F32)
                wfull = tb("wfull_o", [P, PL, H], F32)
                wt = tb("wt_o", [P, 2, PL, H], F32R)
                bias = tb("bias_o", [P, H], F32)
                xb = tb("xb", [P, SUB, H], F32)
                ot = tb("ot", [P, 2, PL, BT], F32R)
                with nc.Block() as block:
                    @block.sync
                    def _(sp):
                        sp.dma_start(raw[:, :, :], Wo.rearrange("(hh p) c -> p hh c", p=P)).then_inc(s["loaded"], 16)
                        sp.dma_start(bias[:, :], bo.rearrange("(o c) -> o c", o=1).broadcast_to([P, H])).then_inc(s["loaded"], 16)

                    @block.tensor
                    def _(pe):
                        pe.wait_ge(s["loaded"], 32)
                        for pl in range(PL):
                            for hh in range(2):
                                last = nc.tensor.transpose(psum[:, pl, hh * P:(hh + 1) * P], raw[:, hh, pl::PL], ident[:, :])
                        last.then_inc(s["wt"], 1)
                        pe.wait_ge(s["wt_lo"], 1)
                        with nc.tensor.Fori(0, NB) as b:
                            pe.wait_ge(s["xb"], b + 1)
                            turn_tensor(xb, 4).then_inc(s["turned"], 1)
                            pe.wait_ge(s["ot_lo"], b + 1)
                            for i in range(SUB):
                                pe.wait_ge(s["added"], b * SUB + i + 1)
                                n = 0
                                for pl in range(PL):
                                    for a, c in PASSES:
                                        last = nc.tensor.matmul(psum[:, i, 0:H], ot[:, a, pl, i * P:(i + 1) * P],
                                                                wt[:, c, pl, :], start=(n == 0), stop=(n == 5))
                                        n += 1
                                last.then_inc(s["summed"], 1)

                    @block.scalar
                    def _(act):
                        act.sem_inc(s["turned"], 1)
                        act.sem_inc(s["summed"], 1)
                        act.wait_ge(s["wt"], 1)
                        nc.scalar.activation(wfull[:, :, :], psum[:, 0:2, 0:H], ACT.Copy).then_inc(s["wfull"], 1)
                        with nc.scalar.Fori(0, NB) as b:
                            act.wait_ge(s["turned"], b + 2)
                            act.wait_ge(s["summed"], b * SUB + 1)
                            nc.scalar.activation(ot[:, 0, :, :], psum[:, 4:6, :], ACT.Copy).then_inc(s["ot_hi"], 1)

                    @block.vector
                    def _(dve):
                        dve.sem_inc(s["added"], SUB)
                        dve.wait_ge(s["loaded"], 32)
                        nc.vector.tensor_tensor(x[:, :, :], x[:, :, :], bias[:, :].unsqueeze(1).broadcast_to([P, TT, H]),
                                                ALU.add).then_inc(s["biased"], 1)
                        dve.wait_ge(s["wfull"], 1)
                        nc.vector.tensor_copy(wt[:, 0, :, :], wfull[:, :, :]).then_inc(s["wt_hi"], 1)
                        dve.wait_ge(s["wt_hi"], 1)
                        nc.vector.tensor_tensor(wt[:, 1, :, :], wfull[:, :, :], as_f32(wt[:, 0, :, :]), ALU.subtract).then_inc(s["wt_lo"], 1)
                        dve.wait_ge(s["biased"], 1)
                        with nc.vector.Fori(0, NB) as b:
                            dve.wait_ge(s["turned"], b + 1)
                            nc.vector.tensor_copy(xb[:, :, :], heads[:, bass.ds(b * SUB, SUB), :]).then_inc(s["xb"], 1)
                            dve.wait_ge(s["ot_hi"], b + 1)
                            nc.vector.tensor_tensor(ot[:, 1, :, :], psum[:, 4:6, :], as_f32(ot[:, 0, :, :]),
                                                    ALU.subtract).then_inc(s["ot_lo"], 1)
                            for i in range(SUB):
                                dve.wait_ge(s["summed"], b * SUB + i + 2)
                                dst = x[:, bass.ds(b * SUB + i, 1), :].rearrange("p o c -> p (o c)")
                                nc.vector.tensor_tensor(dst, psum[:, i, 0:H], dst, ALU.add).then_inc(s["added"], 1)
                            dve.wait_ge(s["added"], (b + 2) * SUB)
                            norm_stats(b)

        NORM = "stats aggr var std rstd xb "
        W_SEMS = "scales x ident turned_s wide turned_c byte turned weight w_hi step value " + " ".join(f"codes{n}" for n in range(3 * NG))
        F_SEMS = NORM + "turned gu product inner_lo down added xt_hi xt_lo tanh square cubic quadratic gelu inner_hi stored"
        Q_SEMS = NORM + ("loaded wt wfull wt_hi wt_lo turned xt_hi xt_lo full unit v_sum v bias_q part_1 part_2 part_3 rest "
                         "part_out0 part_out1 part_out2 part_out3 v_out0 v_out1 v_out2 v_out3")
        A_SEMS = ("stack0 stack1 stack2 max_rows max_loaded ones scored weighted mask exp masked max_read max_scored max_parts "
                  "passed normed max_turned o_copied gathered row_max max_step rden")
        O_SEMS = "xb loaded wt wfull wt_hi wt_lo turned ot_hi ot_lo summed added biased"

        def named(phase, names):
            return {n: outer.enter_context(nc.semaphore(f"{phase}_{n}")) for n in names.split()}

        dequantise(named("dequant", W_SEMS))
        ffn("ffn1", named("ffn1", F_SEMS), False)
        qkv(named("qkv", Q_SEMS))
        attention(named("attn", A_SEMS))
        project(named("proj", O_SEMS))
        ffn("ffn2", named("ffn2", F_SEMS), True)


_INS = ["L0_attn_h", "L0_attn_Wq", "L0_attn_bq", "L0_attn_Wk", "L0_attn_bk", "L0_attn_Wv", "L0_attn_bv", "L0_attn_Wo",
        "L0_attn_bo", "L0_ffn_gate_W_packed", "L0_ffn_gate_scales", "L0_ffn_up_W_packed", "L0_ffn_up_scales",
        "L0_ffn_down_W_packed", "L0_ffn_down_scales"]


def kernel(**inputs):
    import numpy as _np
    import concourse.bacc as _bacc
    from concourse import mybir as _mybir
    from concourse.bass_utils import run_bass_kernel_spmd as _run

    nc = _bacc.Bacc("TRN2", target_bir_lowering=False, num_devices=1)
    arrays, args = {}, []
    for name in _INS:
        a = _np.ascontiguousarray(inputs[name])
        arrays[f"in_{name}"] = a
        args.append(nc.dram_tensor(f"in_{name}", a.shape, _mybir.dt.from_np(a.dtype), kind="ExternalInput").ap())
    args.append(nc.dram_tensor("out", (1, T, H), F32, kind="ExternalOutput").ap())
    build_program(nc, *args)
    r = _run(nc, [arrays], core_ids=[0])
    return r.results[0]["out"]
```

```python
from contextlib import ExitStack

import concourse.bass as bass
from concourse import mybir

F32 = mybir.dt.float32
F32R = mybir.dt.float32r
BF16 = mybir.dt.bfloat16
I32 = mybir.dt.int32
U8 = mybir.dt.uint8
U16 = mybir.dt.uint16
ALU = mybir.AluOpType
ACT = mybir.ActivationFunctionType
AX = mybir.AxisListType

P = 128
T, H, F = 2048, 256, 2048
NH = 16
HD = H // NH
EPS = 1e-5
TT = T // P
BT = 512
NB = T // BT
SUB = BT // P
PL = 2
NQ = F // P
GT = 4
NG = NQ // GT
BLK = 16
GELU_C, GELU_A = 0.7978845608028654, 0.044715
PASSES = ((0, 0), (0, 1), (1, 0))
MASKED = -1e30
CREDIT = 2
START = -3e38

NPAIR = NH // 2
HALF = 64
NPART = 3
Q_PARTS = (0, 0, 0, 1, 1, 2)
K_PARTS = (0, 1, 2, 0, 1, 0)
NKB = T // P
KR = len(Q_PARTS) * HD
SB = 3
SBANKS = 3
MBANKS = 3
PRING = 8
VW = 34


def build_program(nc, h, Wq, bq, Wk, bk, Wv, bv, Wo, bo, gW, gS, uW, uS, dW, dS, out):
    nc.disable_value_cache = True
    outer = ExitStack()

    def tensors(stack, phase):
        return lambda name, shape, dt: stack.enter_context(nc.sbuf_tensor(f"{phase}_{name}", shape, dt))

    with outer:
        sb = tensors(outer, "all")
        x = sb("x", [P, TT, H], F32)
        heads = sb("heads", [P, TT, H], F32)
        w_hi = sb("w_hi", [P, 3 * NG, PL, GT * P], F32R)
        w_lo = sb("w_lo", [P, 3 * NG, PL, GT * P], F32R)
        w_part = (w_hi, w_lo)
        ident = sb("ident", [P, P], F32)
        stats = sb("stats", [P, TT, 6], F32)
        mean_var = sb("mean_var", [P, TT, 2], F32)
        var_eps = sb("var_eps", [P, TT], F32)
        deviation = sb("deviation", [P, TT], F32)
        rstd = sb("rstd", [P, TT], F32)
        psum = outer.enter_context(nc.psum_tensor("psum", [P, 8, BT], F32))
        qk_dram = nc.dram_tensor("qk_parts", (2 * NPART, H, T), BF16, kind="Internal").ap()
        v_dram = nc.dram_tensor("v_rows", (NPAIR, P, NKB, 2 * HD), F32, kind="Internal").ap()

        def as_f32(ap):
            return ap.bitcast(F32)

        def norm_stats(b):
            for i in range(SUB):
                t = b * SUB + i
                last = nc.vector.bn_stats(stats[:, bass.ds(t, 1), :].rearrange("p o c -> p (o c)"),
                                          x[:, bass.ds(t, 1), :].rearrange("p o c -> p (o c)"))
            return last

        def norm_vector(dve, s):
            for t in range(TT):
                last = nc.vector.bn_aggr(mean_var[:, t, :], stats[:, t, :])
            last.then_inc(s["aggr"], 1)
            dve.wait_ge(s["aggr"], 1)
            nc.vector.tensor_scalar(var_eps[:, :], mean_var[:, :, 1], EPS, None, ALU.add).then_inc(s["var"], 1)
            dve.wait_ge(s["std"], 1)
            nc.vector.reciprocal(rstd[:, :], deviation[:, :]).then_inc(s["rstd"], 1)
            dve.wait_ge(s["rstd"], 1)

        def norm_block(dve, s, b, use, xb):
            dve.wait_ge(s["turned"], use + 1)
            for i in range(SUB):
                t = b * SUB + i
                last = nc.vector.tensor_scalar(xb[:, i, :], x[:, bass.ds(t, 1), :].rearrange("p o c -> p (o c)"),
                                               mean_var[:, bass.ds(t, 1), 0], rstd[:, bass.ds(t, 1)],
                                               ALU.subtract, ALU.mult)
            last.then_inc(s["xb"], 1)

        def norm_scalar(act, s):
            act.wait_ge(s["var"], 1)
            nc.scalar.activation(deviation[:, :], var_eps[:, :], ACT.Sqrt).then_inc(s["std"], 1)

        def turn_tensor(xb, bank):
            for pl in range(PL):
                for i in range(SUB):
                    last = nc.tensor.transpose(psum[:, bank + pl, i * P:(i + 1) * P],
                                               xb[:, i, pl::PL], ident[:, :])
            return last

        def dequantise(s):
            with ExitStack() as st:
                tb = tensors(st, "dequant")
                codes = tb("codes", [P, 3 * NG, GT, P], I32)
                scales = tb("scales", [P, 2, NG, GT, P // BLK], F32)
                d_scales = tb("d_scales", [P, 2, F // 32], F32)
                identb = tb("identb", [P, P], BF16)
                byte = tb("byte", [P, 2, GT * P], BF16)
                wide = tb("wide", [P, 2, GT, P], F32)
                turned = tb("turned", [P, 2, GT * P], U16)
                mag = tb("mag", [P, 2, PL, GT * P], U16)
                sign = tb("sign", [P, 2, PL, GT * P], U16)
                low = tb("low", [P, 2, PL, GT * P], BF16)
                weight = tb("weight", [P, 2, PL, GT * P], F32)
                NGR = 3 * NG

                def rows(w):
                    return w.rearrange("(c p two) j -> p c two j", p=P, two=2)

                with nc.Block() as block:
                    @block.sync
                    def _(sp):
                        for m, sc in ((0, gS), (1, uS)):
                            sp.dma_start(scales[:, m, :, :, :].rearrange("p g (c two) b -> p (g c) two b", two=2),
                                         rows(sc)).then_inc(s["scales"], 16)
                        sp.dma_start(d_scales[:, :, :], dS.rearrange("(hh p) b -> p hh b", p=P)).then_inc(s["scales"], 16)
                        for g in range(NG):
                            for m, w in ((0, gW), (1, uW)):
                                sp.dma_start(codes[:, 3 * g + m, :, :].rearrange("p (c two) j -> p c two j", two=2),
                                             rows(w)[:, 2 * g:2 * g + 2]).then_inc(s[f"codes{3 * g + m}"], 16)
                            for c in range(2):
                                sp.dma_start(codes[:, 3 * g + 2, 2 * c:2 * c + 2, :],
                                             dW[:, (2 * g + c) * P:(2 * g + c + 1) * P].rearrange("(hh p) j -> p hh j", p=P)
                                             ).then_inc(s[f"codes{3 * g + 2}"], 16)
                        for t in range(0, TT, 4):
                            sp.dma_start(x[:, t:t + 4, :], h[0, t * P:(t + 4) * P, :].rearrange("(t p) c -> p t c", p=P)
                                         ).then_inc(s["x"], 16)
                        sp.wait_ge(s["x"], 16 * (TT // 4))

                    @block.gpsimd
                    def _(pool):
                        nc.gpsimd.memset(ident[:, :], 0.0).then_inc(s["ident"], 1)
                        pool.wait_ge(s["ident"], 1)
                        nc.gpsimd.affine_select(out=ident[:, :], in_=ident[:, :], compare_op=ALU.not_equal, fill=1.0,
                                                base=0, pattern=[[-1, P]], channel_multiplier=1).then_inc(s["ident"], 1)
                        pool.wait_ge(s["ident"], 2)
                        nc.gpsimd.tensor_copy(identb[:, :], ident[:, :]).then_inc(s["ident"], 1)
                        for n in range(NGR):
                            pool.wait_ge(s["w_hi"], n + 1)
                            nc.gpsimd.tensor_tensor(w_lo[:, n], weight[:, n % 2], as_f32(w_hi[:, n]), ALU.subtract).then_inc(s["w_lo"], 1)

                    @block.scalar
                    def _(act):
                        def widen(n):
                            g, m = divmod(n, 3)
                            if n >= 2:
                                act.wait_ge(s["turned_s"], n - 1)
                            src = (scales[:, m, g, :, :] if m < 2 else
                                   d_scales[:, :, 16 * g:16 * (g + 1)].rearrange("p hh (c b) -> p c hh b", c=2))
                            to = wide[:, n % 2, :, :].rearrange("p i (a b) -> p i a b", b=BLK)
                            if m < 2:
                                nc.scalar.activation(to, src.unsqueeze(3).broadcast_to([P, GT, P // BLK, BLK]),
                                                     ACT.Copy).then_inc(s["wide"], 2)
                            else:
                                for c in range(2):
                                    nc.scalar.activation(to[:, 2 * c:2 * c + 2], src[:, c].unsqueeze(3).broadcast_to([P, 2, P // BLK, BLK]),
                                                         ACT.Copy).then_inc(s["wide"], 1)

                        for n in range(NGR + 1):
                            if n < NGR:
                                act.wait_ge(s[f"codes{n}"], 16 if n % 3 < 2 else 32)
                                if n >= 2:
                                    act.wait_ge(s["turned_c"], n - 1)
                                nc.scalar.activation(byte[:, n % 2, :],
                                                     codes[:, n, :, :].rearrange("p a b -> p (a b)").bitcast(U8)[:, ::4],
                                                     ACT.Copy).then_inc(s["byte"], 1)
                                if n == 0:
                                    act.wait_ge(s["scales"], 48)
                                widen(n)
                                act.wait_ge(s["turned_c"], n + 1)
                                if n >= 2:
                                    act.wait_ge(s["weight"], n - 1)
                                nc.scalar.activation(turned[:, n % 2, :], psum[:, n % 2, 0:BT // 2].bitcast(BF16),
                                                     ACT.Copy).then_inc(s["turned"], 1)
                            if n >= 1:
                                act.wait_ge(s["weight"], n)
                                nc.scalar.activation(w_hi[:, n - 1, :, :], weight[:, (n - 1) % 2, :, :],
                                                     ACT.Copy).then_inc(s["w_hi"], 1)

                    @block.tensor
                    def _(pe):
                        pe.wait_ge(s["ident"], 3)
                        for n in range(NGR):
                            pe.wait_ge(s["byte"], n + 1)
                            if n >= 2:
                                pe.wait_ge(s["turned"], n - 1)
                            for i in range(GT):
                                last = nc.tensor.transpose(psum[:, n % 2, i * HALF:(i + 1) * HALF].bitcast(BF16),
                                                           byte[:, n % 2, i * P:(i + 1) * P], identb[:, :])
                            last.then_inc(s["turned_c"], 1)
                            pe.wait_ge(s["wide"], 2 * n + 2)
                            if n >= 2:
                                pe.wait_ge(s["weight"], n - 1)
                            for i in range(GT):
                                last = nc.tensor.transpose(psum[:, 2 + n % 2, i * P:(i + 1) * P], wide[:, n % 2, i, :],
                                                           ident[:, :])
                            last.then_inc(s["turned_s"], 1)

                    @block.vector
                    def _(dve):
                        def own(instruction, count):
                            instruction.then_inc(s["step"], 1)
                            dve.wait_ge(s["step"], count)

                        for n in range(NGR):
                            code, m, sg, lw = turned[:, n % 2, :], mag[:, n % 2], sign[:, n % 2], low[:, n % 2]
                            dve.wait_ge(s["turned"], n + 1)
                            nc.vector.tensor_scalar(m[:, 0, :], code, 0xF8, 6, ALU.bitwise_or, ALU.logical_shift_left)
                            nc.vector.tensor_scalar(sg[:, 0, :], code, 0x08, 12, ALU.bitwise_and, ALU.logical_shift_left)
                            nc.vector.tensor_scalar(sg[:, 1, :], code, 0x80, 8, ALU.bitwise_and, ALU.logical_shift_left)
                            own(nc.vector.tensor_scalar(m[:, 1, :], code, 0x70, 0xF80, ALU.bitwise_and, ALU.bitwise_or), 3 * n + 1)
                            own(nc.vector.tensor_scalar(m[:, 1, :], m[:, 1, :], 2, None, ALU.logical_shift_left), 3 * n + 2)
                            g8 = m.bitcast(BF16)
                            own(nc.vector.tensor_scalar(lw, g8, 2.0, -0.25, ALU.mult, ALU.add), 3 * n + 3)
                            nc.vector.tensor_tensor(g8, g8, lw, ALU.min).then_inc(s["value"], 1)
                            dve.wait_ge(s["value"], 2 * n + 1)
                            nc.vector.tensor_tensor(m, m, sg, ALU.bitwise_or).then_inc(s["value"], 1)
                            dve.wait_ge(s["value"], 2 * n + 2)
                            dve.wait_ge(s["turned_s"], n + 1)
                            if n >= 2:
                                dve.wait_ge(s["w_lo"], n - 1)
                            nc.vector.scalar_tensor_tensor(weight[:, n % 2], g8, 4.0,
                                                           psum[:, 2 + n % 2, :].unsqueeze(1).broadcast_to([P, PL, BT]),
                                                           ALU.mult, ALU.mult).then_inc(s["weight"], 1)
                        dve.wait_ge(s["x"], 16 * NB)
                        for b in range(NB):
                            norm_stats(b)

        def ffn(phase, s, store):
            with ExitStack() as st:
                tb = tensors(st, phase)
                xb = tb("xb", [P, SUB, H], F32)
                xt = tb("xt", [P, 2, 2, PL, BT], F32R)
                inner = tb("inner", [P, 2, 2, BT], F32R)
                arg = tb("arg", [P, 2, BT], F32)
                act_out = tb("act_out", [P, 2, BT], F32)
                ACC = 6
                SPLIT = NQ // 2

                def loop(engine, block_steps):
                    with engine.Fori(0, NB // 2) as it:
                        block_steps(it * 2, 0, it * 2 + 1)
                        block_steps(it * 2 + 1, 1, it * -2 + 2)

                with nc.Block() as block:
                    @block.tensor
                    def _(pe):
                        def turn(use):
                            pe.wait_ge(s["xb"], use + 1)
                            if not isinstance(use, int):
                                pe.wait_ge(s["xt_lo"], use)
                            turn_tensor(xb, 4).then_inc(s["turned"], 1)

                        def gate_up(b, k, q):
                            pe.wait_ge(s["product"], b * NQ + q + 1)
                            g, o = q // GT, (q % GT) * P
                            for m in range(2):
                                n = 0
                                for pl in range(PL):
                                    for a, c in PASSES:
                                        last = nc.tensor.matmul(psum[:, 2 * m + q % 2, :],
                                                                w_part[a][:, 3 * g + m, pl, o:o + P], xt[:, k, c, pl, :],
                                                                start=(n == 0), stop=(n == 5))
                                        n += 1
                            last.then_inc(s["gu"], 1)

                        def down(b, q):
                            pe.wait_ge(s["inner_lo"], b * NQ + q + 1 + CREDIT)
                            if q == 0:
                                pe.wait_ge(s["added"], b + 1)
                            c, pl = divmod(q, 2)
                            for i in range(SUB):
                                for n, (a, e) in enumerate(PASSES):
                                    last = nc.tensor.matmul(psum[:, ACC + i // 2, (i % 2) * H:(i % 2 + 1) * H],
                                                            inner[:, a, q % 2, i * P:(i + 1) * P],
                                                            w_part[e][:, 3 * (c // 2) + 2, pl, (c % 2) * H:(c % 2 + 1) * H],
                                                            start=(q == 0 and n == 0 and i % 2 == 0),
                                                            stop=(q == NQ - 1 and n == 2), skip_group_check=True)
                            last.then_inc(s["down"], 1)

                        def block_steps(b, k, following):
                            pe.wait_ge(s["xt_lo"], b + 1)
                            for q in range(NQ):
                                gate_up(b, k, q)
                                if q == SPLIT:
                                    turn(b + 1)
                                if q >= 2:
                                    down(b, q - 2)
                                elif k == 1:
                                    down(b - 1, NQ - 2 + q)
                            if k == 1:
                                down(b, NQ - 2)
                                down(b, NQ - 1)

                        turn(0)
                        loop(nc.tensor, block_steps)

                    @block.scalar
                    def _(act):
                        norm_scalar(act, s)

                        def split(use, k):
                            act.wait_ge(s["turned"], use + 2)
                            nc.scalar.activation(xt[:, k, 0, :, :], psum[:, 4:6, :], ACT.Copy).then_inc(s["xt_hi"], 1)

                        def high_part(b, q):
                            u = q % 2
                            n = b * NQ + q
                            act.wait_ge(s["product"], n + 1 + CREDIT)
                            act.wait_ge(s["down"], n + 1)
                            nc.scalar.activation(inner[:, 0, u, :], act_out[:, u, :], ACT.Copy).then_inc(s["inner_hi"], 1)

                        def block_steps(b, k, following):
                            for q in range(NQ):
                                n = b * NQ + q
                                u = q % 2
                                act.wait_ge(s["gu"], n + 1)
                                act.wait_ge(s["tanh"], n + 1)
                                nc.scalar.activation(arg[:, u, :], psum[:, u, :], ACT.Square).then_inc(s["square"], 1)
                                if q >= 1:
                                    high_part(b, q - 1)
                                elif k == 1:
                                    high_part(b - 1, NQ - 1)
                                act.wait_ge(s["cubic"], n + 1)
                                act.wait_ge(s["inner_lo"], n + 1)
                                nc.scalar.activation(act_out[:, u, :], arg[:, u, :], ACT.Tanh,
                                                     scale=GELU_C).then_inc(s["tanh"], 1)
                                if q == SPLIT + 1:
                                    split(b + 1, 1 - k)
                            if k == 1:
                                high_part(b, NQ - 1)

                        act.sem_inc(s["tanh"], CREDIT)
                        split(0, 0)
                        loop(nc.scalar, block_steps)

                    @block.vector
                    def _(dve):
                        dve.sem_inc(s["product"], CREDIT)
                        dve.sem_inc(s["inner_lo"], CREDIT)
                        dve.sem_inc(s["added"], 1)
                        norm_vector(dve, s)

                        def split(use, k):
                            dve.wait_ge(s["xt_hi"], use + 1)
                            nc.vector.tensor_tensor(xt[:, k, 1, :, :], psum[:, 4:6, :], as_f32(xt[:, k, 0, :, :]),
                                                    ALU.subtract).then_inc(s["xt_lo"], 1)

                        def low_part(b, q):
                            u = q % 2
                            dve.wait_ge(s["inner_hi"], b * NQ + q + 1)
                            nc.vector.tensor_tensor(inner[:, 1, u, :], act_out[:, u, :], as_f32(inner[:, 0, u, :]),
                                                    ALU.subtract).then_inc(s["inner_lo"], 1)

                        def add(b):
                            dve.wait_ge(s["down"], (b + 1) * NQ + CREDIT)
                            for j in range(2):
                                dst = x[:, bass.ds(b * SUB + 2 * j, 2), :].rearrange("p a c -> p (a c)")
                                last = nc.vector.scalar_tensor_tensor(dst, psum[:, ACC + j, :], 0.5, dst, ALU.mult, ALU.add)
                            last.then_inc(s["added"], 1)
                            if not store:
                                dve.wait_ge(s["added"], b + 2)

                        def block_steps(b, k, following):
                            for q in range(NQ):
                                n = b * NQ + q
                                u = q % 2
                                if q == 2 and k == 1:
                                    add(b - 1)
                                if q == 4 and k == 1 and not store:
                                    norm_stats(b - 1)
                                dve.wait_ge(s["square"], n + 1)
                                nc.vector.tensor_scalar(arg[:, u, :], arg[:, u, :], GELU_A, 1.0, ALU.mult,
                                                        ALU.add).then_inc(s["quadratic"], 1)
                                dve.wait_ge(s["quadratic"], n + 1)
                                nc.vector.tensor_tensor(arg[:, u, :], arg[:, u, :], psum[:, u, :],
                                                        ALU.mult).then_inc(s["cubic"], 1)
                                if q >= 1:
                                    low_part(b, q - 1)
                                elif k == 1:
                                    low_part(b - 1, NQ - 1)
                                if q == SPLIT - 2:
                                    norm_block(dve, s, following, b + 1, xb)
                                if q == SPLIT + 2:
                                    split(b + 1, 1 - k)
                                dve.wait_ge(s["tanh"], n + 1 + CREDIT)
                                nc.vector.scalar_tensor_tensor(act_out[:, u, :], act_out[:, u, :], 1.0, psum[:, u, :],
                                                               ALU.add, ALU.mult).then_inc(s["gelu"], 1)
                                dve.wait_ge(s["gelu"], n + 1)
                                nc.vector.scalar_tensor_tensor(act_out[:, u, :], act_out[:, u, :], 0.5, psum[:, 2 + u, :],
                                                               ALU.mult, ALU.mult).then_inc(s["product"], 1)
                            if k == 1:
                                low_part(b, NQ - 1)
                                add(b)
                                if not store:
                                    norm_stats(b)

                        norm_block(dve, s, 0, 0, xb)
                        split(0, 0)
                        loop(nc.vector, block_steps)

                    @block.gpsimd
                    def _(pool):
                        pool.sem_inc(s["down"], CREDIT)
                        pool.sem_inc(s["turned"], 1)

                    @block.sync
                    def _(sp):
                        if store:
                            with nc.sync.Fori(0, NB) as b:
                                sp.wait_ge(s["added"], b + 2)
                                sp.dma_start(out[0, bass.ds(b * BT, BT), :].rearrange("(t p) c -> p t c", p=P),
                                             x[:, bass.ds(b * SUB, SUB), :]).then_inc(s["stored"], 16)
                            sp.wait_ge(s["stored"], 16 * NB)

        def qkv(s):
            with ExitStack() as st:
                tb = tensors(st, "qkv")
                raw = tb("raw", [P, 3, 2, H], F32)
                wt = tb("wt", [P, 2, 3, PL, H], F32R)
                wfull = tb("wfull", [P, 3, PL, H], F32)
                bias = tb("bias", [P, 2, 2], F32)
                bias_v = tb("bias_v", [P, H], F32)
                xb = tb("xb", [P, SUB, H], F32)
                xt = tb("xt", [P, 2, 2, PL, BT], F32R)
                NU = 4
                full = tb("full", [P, NU, BT], F32)
                rest = tb("rest", [P, NU, BT], F32)
                parts = tb("parts", [P, NU, NPART, BT], BF16)
                rows_v = tb("rows_v", [P, SUB, H], F32)
                bias_q = tb("bias_q", [P, 2], F32)
                SCALE = HD ** -0.5

                def loop(engine, block_steps):
                    with engine.Fori(0, NB // 2) as it:
                        block_steps(it * 2, 0, it * 2 + 1)
                        block_steps(it * 2 + 1, 1, it * -2 + 2)

                with nc.Block() as block:
                    @block.sync
                    def _(sp):
                        for m, w in enumerate((Wq, Wk, Wv)):
                            sp.dma_start(raw[:, m, :, :], w.rearrange("(hh p) c -> p hh c", p=P)).then_inc(s["loaded"], 16)
                        for m, b_ in enumerate((bq, bk)):
                            sp.dma_start(bias[:, m, :], b_.rearrange("(hh p) -> p hh", p=P),
                                         allow_slow_non_contiguous=True).then_inc(s["loaded"], 16)
                        sp.dma_start(bias_v[:, :], bv.rearrange("(o c) -> o c", o=1).broadcast_to([P, H])).then_inc(s["loaded"], 16)

                        def block_steps(b, k, following):
                            for u in range(NU):
                                kind, half = divmod(u, 2)
                                sp.wait_ge(s["part_3"], b * NU + u + 1 + NU)
                                sp.dma_start(qk_dram[NPART * kind:NPART * (kind + 1), half * P:(half + 1) * P, bass.ds(b * BT, BT)]
                                             .rearrange("a p t -> p a t"), parts[:, u, :, :]).then_inc(s[f"part_out{u}"], 16)
                            sp.wait_ge(s["v"], (b + 1) * SUB + CREDIT)
                            for i in range(SUB):
                                sp.dma_start(v_dram[:, :, bass.ds(b * SUB + i, 1), :].rearrange("r p o c -> p r (o c)"),
                                             rows_v[:, i, :].rearrange("p (r c) -> p r c", c=2 * HD)).then_inc(s[f"v_out{i}"], 16)

                        loop(nc.sync, block_steps)
                        for u in range(NU):
                            sp.wait_ge(s[f"part_out{u}"], 16 + 16 * NB)
                            sp.wait_ge(s[f"v_out{u}"], 16 + 16 * NB)

                    @block.tensor
                    def _(pe):
                        def turn(use):
                            pe.wait_ge(s["xb"], use + 1)
                            if not isinstance(use, int):
                                pe.wait_ge(s["xt_lo"], use)
                            turn_tensor(xb, 4).then_inc(s["turned"], 1)

                        def block_steps(b, k, following):
                            def rows_of_v(i):
                                pe.wait_ge(s["v"], b * SUB + i + 1)
                                n = 0
                                for pl in range(PL):
                                    for a, c in PASSES:
                                        last = nc.tensor.matmul(psum[:, 6 + i % 2, 0:H], xt[:, k, a, pl, i * P:(i + 1) * P],
                                                                wt[:, c, 2, pl, :], start=(n == 0), stop=(n == 5))
                                        n += 1
                                last.then_inc(s["v_sum"], 1)

                            pe.wait_ge(s["xt_lo"], b + 1)
                            for u in range(NU):
                                kind, half = divmod(u, 2)
                                pe.wait_ge(s["full"], b * NU + u + 1)
                                n = 0
                                for pl in range(PL):
                                    for a, c in PASSES:
                                        last = nc.tensor.matmul(psum[:, u, :], wt[:, a, kind, pl, half * P:(half + 1) * P],
                                                                xt[:, k, c, pl, :], start=(n == 0), stop=(n == 5))
                                        n += 1
                                last.then_inc(s["unit"], 1)
                                rows_of_v(u)
                                if u == 1:
                                    turn(b + 1)

                        turn(0)
                        pe.wait_ge(s["loaded"], 96)
                        for m in range(3):
                            if m == 2:
                                pe.wait_ge(s["wfull"], 1)
                            for pl in range(PL):
                                for hh in range(2):
                                    last = nc.tensor.transpose(psum[:, 2 * (m % 2) + pl, hh * P:(hh + 1) * P],
                                                               raw[:, m, hh, pl::PL], ident[:, :])
                            last.then_inc(s["wt"], 1)
                        pe.wait_ge(s["wt_lo"], 3)
                        loop(nc.tensor, block_steps)

                    @block.scalar
                    def _(act):
                        def split(use, k):
                            act.wait_ge(s["turned"], use + 2)
                            nc.scalar.activation(xt[:, k, 0, :, :], psum[:, 4:6, :], ACT.Copy).then_inc(s["xt_hi"], 1)

                        def part(b, u, j):
                            n = b * NU + u
                            if j == 0:
                                act.wait_ge(s["full"], n + 1 + NU)
                                act.wait_ge(s[f"part_out{u}"], (b + 1) * 16)
                            else:
                                act.wait_ge(s["rest"], n + 1)
                            nc.scalar.activation(parts[:, u, j, :], (full if j == 0 else rest)[:, u, :],
                                                 ACT.Copy).then_inc(s[f"part_{j + 1}"], 1)

                        def block_steps(b, k, following):
                            for u in range(NU):
                                kind, half = divmod(u, 2)
                                act.wait_ge(s["unit"], b * NU + u + 1)
                                act.wait_ge(s["part_3"], b * NU + u + 1)
                                nc.scalar.activation(full[:, u, :], psum[:, u, :], ACT.Identity,
                                                     scale=SCALE if kind == 0 else 1.0,
                                                     bias=bias_q[:, half:half + 1] if kind == 0 else bias[:, 1, half:half + 1]
                                                     ).then_inc(s["full"], 1)
                                part(b, u, 0)
                                if u == 2:
                                    split(b + 1, 1 - k)
                                if u:
                                    part(b, u - 1, 1)
                            part(b, NU - 1, 1)

                        norm_scalar(act, s)
                        split(0, 0)
                        act.wait_ge(s["loaded"], 96)
                        nc.scalar.activation(bias_q[:, :], bias[:, 0, :], ACT.Copy, scale=SCALE).then_inc(s["bias_q"], 1)
                        for m in range(3):
                            act.wait_ge(s["wt"], m + 1)
                            nc.scalar.activation(wfull[:, m, :, :], psum[:, 2 * (m % 2):2 * (m % 2) + 2, 0:H], ACT.Copy).then_inc(s["wfull"], 1)
                        act.wait_ge(s["bias_q"], 1)
                        act.sem_inc(s["full"], NU)
                        loop(nc.scalar, block_steps)

                    @block.vector
                    def _(dve):
                        def split(use, k):
                            dve.wait_ge(s["xt_hi"], use + 1)
                            nc.vector.tensor_tensor(xt[:, k, 1, :, :], psum[:, 4:6, :], as_f32(xt[:, k, 0, :, :]),
                                                    ALU.subtract).then_inc(s["xt_lo"], 1)

                        def lesser(b, u, j):
                            n = b * NU + u
                            dve.wait_ge(s[f"part_{j + 1}"], n + 1)
                            if j == 0:
                                nc.vector.tensor_tensor(rest[:, u, :], full[:, u, :], parts[:, u, 0, :], ALU.subtract).then_inc(s["rest"], 1)
                            else:
                                nc.vector.tensor_tensor(parts[:, u, 2, :], rest[:, u, :], parts[:, u, 1, :], ALU.subtract).then_inc(s["part_3"], 1)

                        def block_steps(b, k, following):
                            norm_block(dve, s, following, b + 1, xb)
                            for u in range(NU):
                                lesser(b, u, 0)
                                dve.wait_ge(s["v_sum"], b * SUB + u + 1)
                                dve.wait_ge(s[f"v_out{u}"], (b + 1) * 16)
                                nc.vector.tensor_tensor(rows_v[:, u, :], psum[:, 6 + u % 2, 0:H], bias_v[:, :],
                                                        ALU.add).then_inc(s["v"], 1)
                                if u == 2:
                                    split(b + 1, 1 - k)
                                if u:
                                    lesser(b, u - 1, 1)
                            lesser(b, NU - 1, 1)

                        dve.sem_inc(s["v"], CREDIT)
                        dve.sem_inc(s["part_3"], NU)
                        norm_vector(dve, s)
                        norm_block(dve, s, 0, 0, xb)
                        split(0, 0)
                        for m in range(3):
                            dve.wait_ge(s["wfull"], m + 1)
                            nc.vector.tensor_copy(wt[:, 0, m, :, :], wfull[:, m, :, :]).then_inc(s["wt_hi"], 1)
                            dve.wait_ge(s["wt_hi"], m + 1)
                            nc.vector.tensor_tensor(wt[:, 1, m, :, :], wfull[:, m, :, :], as_f32(wt[:, 0, m, :, :]),
                                                    ALU.subtract).then_inc(s["wt_lo"], 1)
                        loop(nc.vector, block_steps)

                    @block.gpsimd
                    def _(pool):
                        pool.sem_inc(s["turned"], 1)
                        for u in range(NU):
                            pool.sem_inc(s[f"part_out{u}"], 16)
                            pool.sem_inc(s[f"v_out{u}"], 16)

        def attention(s):
            steps = [(qt, kb) for qt in range(NB) for kb in range(0, SUB * (qt + 1), 2)]
            NS = len(steps)
            NT = 4 * NS
            chunks = [(i, c) for i in range(TT) for c in range(i // SUB + 1)]
            NM = 2 * len(chunks)
            LEAD = NS - 3
            quota = [len(chunks) * min(d + 1, LEAD) // LEAD for d in range(NS)]
            S0, M0, O0, X0 = 0, 3, 6, 7

            def first_query(qt, kb):
                at = max(0, P * (kb - SUB * qt))
                return 0 if (qt, kb) == (0, 1) else at

            masks = [(d, 2 * k + hd) for d, (qt, kb) in enumerate(steps) if kb >= SUB * qt for k in range(2) for hd in range(2)]
            NMASK = len(masks)

            with ExitStack() as st:
                tb = tensors(st, "attn")
                stack = tb("stack", [P, SB, 2, 2, T], BF16)
                prob = tb("prob", [P, PRING, BT], F32)
                vals = tb("vals", [P, SB, NKB, VW], F32)
                o_sb = tb("o_sb", [P, 2, BT], F32)
                pick = tb("pick", [P, VW], F32)
                mask = tb("mask", [P, BT], BF16)
                junk = tb("junk", [P, 2, BT], BF16)
                part_max = tb("part_max", [P, 2, TT, NB], F32)
                row_max = tb("row_max", [P, 2, TT], F32)
                max_parts = tb("max_parts", [P, 2, NPART, TT], BF16)
                max_rows = tb("max_rows", [2 * NPART * TT, P], BF16)
                spare = stats[:, :, :].rearrange("p t c -> p (t c)")
                identb = spare[:, 0:P // 2].bitcast(BF16)
                max_rest = spare[:, P // 2:P // 2 + 2 * TT].rearrange("p (a t) -> p a t", t=TT)
                rden = tb("rden", [P, SUB, 2], F32)

                def alone(engine, s):
                    engine.sem_inc(s["passed"], 1)

                def q_of(b, hd):
                    return stack[:, b, hd, 0, :]

                def k_of(b, hd):
                    return stack[:, b, hd, 1, :]

                def loop(engine, body):
                    body(0, 0, 0)
                    with engine.Fori(0, (NPAIR - 2) // SB) as it:
                        for j in range(1, SB + 1):
                            body(it * SB + j, it, j)
                    body(NPAIR - 1, NPAIR // SB, (NPAIR - 1) % SB)

                def first(p):
                    return isinstance(p, int) and p == 0

                def last_pair(p):
                    return isinstance(p, int) and p == NPAIR - 1

                assert SBANKS == SB and MBANKS == SB

                CUTS = (0, 3, 5, 8, 10)

                def slot(items, k):
                    return items[len(items) * CUTS[k] // 10:len(items) * CUTS[k + 1] // 10]

                def maxima_of(d):
                    return [(m, hd) for m in range(quota[d - 1] if d else 0, quota[d]) for hd in range(2)]

                def ended(d):
                    return steps[d][0] if d == NS - 1 or steps[d + 1][0] != steps[d][0] else None

                LOADS = 2 * 6 + 1

                def loaded(it, j):
                    return (it + j // SB + 1) * LOADS * 16

                with nc.Block() as block:
                    @block.sync
                    def _(sp):
                        def load(p, b):
                            for hd in range(2):
                                rows = bass.ds(p * 2 * HD + hd * HD, HD)
                                for j, n, part in ((0, 3, 0), (3, 2, 1), (5, 1, 2)):
                                    sp.dma_start(q_of(b, hd)[j * HD:(j + n) * HD, :],
                                                 qk_dram[part, rows, :].unsqueeze(0).broadcast_to([n, HD, T])).then_inc(s[f"stack{b}"], 16)
                                for j, n in ((0, 3), (3, 2), (5, 1)):
                                    sp.dma_start(k_of(b, hd)[j * HD:(j + n) * HD, :],
                                                 qk_dram[NPART:NPART + n, rows, :]).then_inc(s[f"stack{b}"], 16)
                            sp.dma_start(vals[:, b, :, 1:1 + 2 * HD], v_dram[bass.ds(p, 1), :, :, :].rearrange("o p k c -> p (o k) c")
                                         ).then_inc(s[f"stack{b}"], 16)

                        def max_row(p, b):
                            sp.wait_ge(s["max_rows"], p + 1)
                            for hd in range(2):
                                sp.dma_start(q_of(b, hd)[KR:KR + NPART, :], max_rows[NPART * hd * TT:NPART * (hd + 1) * TT, :]
                                             ).then_inc(s["max_loaded"], 16)

                        def pair(p, it, j):
                            if not (first(p) or last_pair(p)):
                                sp.wait_ge(s["weighted"], (p - 1) * NS + CREDIT)
                                load(p + 1, (j + 1) % SB)
                            max_row(p, j % SB)

                        load(0, 0)
                        load(1, 1)
                        loop(nc.sync, pair)

                    @block.gpsimd
                    def _(pool):
                        nc.gpsimd.memset(part_max[:, :, :, :], START).then_inc(s["mask"], 1)
                        nc.gpsimd.tensor_copy(identb[:, :], ident[:, :]).then_inc(s["ones"], 1)
                        nc.gpsimd.memset(mask[:, :], 0.0).then_inc(s["mask"], 1)
                        nc.gpsimd.memset(pick[:, :], 0.0).then_inc(s["mask"], 1)
                        pool.wait_ge(s["mask"], 3)
                        nc.gpsimd.affine_select(out=mask[:, BT - P:BT], in_=mask[:, BT - P:BT], compare_op=ALU.is_ge, fill=MASKED,
                                                base=0, pattern=[[-1, P]], channel_multiplier=1).then_inc(s["mask"], 1)
                        n = 4
                        for hd, (first, den) in enumerate(((1, 0), (HD - 1, 2 * HD - 1))):
                            for k in range(2):
                                row = 32 * (2 * hd + k)
                                for cols, r in ((pick[:, hd * HD:(hd + 1) * HD], row + first), (pick[:, 2 * HD + hd:2 * HD + hd + 1], row + den)):
                                    pool.wait_ge(s["mask"], n)
                                    nc.gpsimd.affine_select(out=cols, in_=cols, compare_op=ALU.not_equal, fill=1.0, base=-r,
                                                            pattern=[[-1, cols.shape[1]]], channel_multiplier=1).then_inc(s["mask"], 1)
                                    n += 1
                        nc.gpsimd.memset(vals[:, :, :, 0:1], 1.0).then_inc(s["ones"], 1)
                        nc.gpsimd.memset(vals[:, :, :, VW - 1:VW], 1.0).then_inc(s["ones"], 1)

                        def pair(p, it, j):
                            for n, (d, j) in enumerate(masks):
                                qt, kb = steps[d]
                                kb += j // 2
                                at = first_query(qt, kb)
                                wide = 2 * P if (qt, kb) == (0, 1) else P
                                t = prob[:, (4 * d + j) % PRING, at:at + wide]
                                pool.wait_ge(s["exp"], p * NT + 4 * d + j + 1 + SBANKS)
                                alone(pool, s)
                                nc.gpsimd.affine_select(out=t, in_=t, compare_op=ALU.is_ge, fill=0.0, base=P - wide,
                                                        pattern=[[1, wide]], channel_multiplier=-1).then_inc(s["masked"], 1)

                        loop(nc.gpsimd, pair)

                    @block.tensor
                    def _(pe):

                        def score(p, b, d, j):
                            k, hd = divmod(j, 2)
                            qt, kb = steps[d]
                            at = first_query(qt, kb + k)
                            n = 4 * d + j
                            rows = slice(0, KR + NPART)
                            pe.wait_ge(s["exp"], p * NT + n + 1)
                            nc.tensor.matmul(psum[:, S0 + (b * NT + n) % SBANKS, at:BT], k_of(b, hd)[rows, (kb + k) * P:(kb + k + 1) * P],
                                             q_of(b, hd)[rows, qt * BT + at:(qt + 1) * BT], start=True, stop=True).then_inc(s["scored"], 1)

                        def maxima(p, b, m, hd):
                            i, c = chunks[m]
                            cols = BT if c < i // SUB else P * (i % SUB + 1)
                            pe.wait_ge(s["max_read"], p * NM + 2 * m + hd + 1)
                            nc.tensor.matmul(psum[:, M0 + (b * NM + 2 * m + hd) % MBANKS, 0:cols], q_of(b, hd)[0:KR, i * P:(i + 1) * P],
                                             k_of(b, hd)[0:KR, c * BT:c * BT + cols], start=True, stop=True).then_inc(s["max_scored"], 1)

                        def turn_max(p):
                            pe.wait_ge(s["max_parts"], p + 1)
                            if not first(p):
                                pe.wait_ge(s["normed"], p * NB)
                            alone(pe, s)
                            nc.tensor.transpose(psum[0:2 * NPART * TT, X0, 0:HALF].bitcast(BF16),
                                                max_parts[:, :, :, :].rearrange("p a b c -> p (a b c)"), identb[:, :]).then_inc(s["max_turned"], 1)

                        def weigh(p, b, d):
                            qt, kb = steps[d]
                            pe.wait_ge(s["exp"], p * NT + 4 * d + 4 + SBANKS)
                            done = sum(1 for e, _ in masks if e <= d)
                            if kb >= SUB * qt:
                                pe.wait_ge(s["masked"], p * NMASK + done)
                            if kb == 0:
                                pe.wait_ge(s["o_copied"], p * NB + qt + CREDIT)
                            for hd in range(2):
                                for k in range(2):
                                    at = first_query(qt, kb + k)
                                    r = 32 * (2 * hd + k)
                                    last = nc.tensor.matmul(psum[r:r + 32, O0, at:BT], vals[:, b, kb + k, 2 * hd:2 * hd + 32],
                                                            prob[:, (4 * d + 2 * k + hd) % PRING, at:BT], start=(kb == 0),
                                                            stop=(kb == SUB * (qt + 1) - 2), skip_group_check=True)
                            last.then_inc(s["weighted"], 1)

                        def gather(p, qt, following):
                            pe.wait_ge(s["o_copied"], p * NB + qt + 1 + CREDIT)
                            pe.wait_ge(s["max_rows"], p + 1 + following)
                            pe.wait_ge(s["normed"], p * NB + qt + 1)
                            for i in range(SUB):
                                last = nc.tensor.matmul(psum[:, X0, i * VW:(i + 1) * VW], o_sb[:, qt % 2, i * P:(i + 1) * P], pick[:, :],
                                                        start=True, stop=True)
                            last.then_inc(s["gathered"], 1)

                        def pair(p, it, j):
                            b, nb = j % SB, (j + 1) % SB
                            pe.wait_ge(s["max_loaded"], 32 * (p + 1))
                            if not last_pair(p):
                                pe.wait_ge(s[f"stack{nb}"], loaded(it, j + 1))
                            for d in range(NS):
                                for k in range(4):
                                    score(p, b, d, k)
                                    if not last_pair(p):
                                        for m, hd in slot(maxima_of(d), k):
                                            maxima(p + 1, nb, m, hd)
                                    if k == 2:
                                        if d >= 2 and ended(d - 2) is not None:
                                            gather(p, ended(d - 2), 0)
                                        elif d == 1 and not first(p):
                                            gather(p - 1, NB - 1, 1)
                                    if k == 3:
                                        if d >= 1:
                                            weigh(p, b, d - 1)
                                        elif not first(p):
                                            weigh(p - 1, (j - 1) % SB, NS - 1)
                                if d == LEAD and not last_pair(p):
                                    turn_max(p + 1)

                        pe.wait_ge(s["stack0"], loaded(0, 0))
                        for m in range(len(chunks)):
                            for hd in range(2):
                                maxima(0, 0, m, hd)
                        pe.wait_ge(s["ones"], 4)
                        turn_max(0)
                        pe.wait_ge(s["mask"], 12)
                        loop(nc.tensor, pair)
                        weigh(NPAIR - 1, (NPAIR - 1) % SB, NS - 1)
                        gather(NPAIR - 1, NB - 1, 0)

                    @block.scalar
                    def _(act):
                        def copy_max(p):
                            act.wait_ge(s["max_turned"], p + 1)
                            act.wait_ge(s["max_loaded"], 32 * p)
                            nc.scalar.activation(max_rows[:, :], psum[0:2 * NPART * TT, X0, 0:HALF].bitcast(BF16), ACT.Copy).then_inc(s["max_rows"], 1)

                        def copy_out(p, qt):
                            act.wait_ge(s["weighted"], p * NS + sum(1 for e in steps if e[0] <= qt) + CREDIT)
                            act.wait_ge(s["gathered"], p * NB + qt + 1)
                            nc.scalar.activation(o_sb[:, qt % 2, :], psum[:, O0, :], ACT.Copy).then_inc(s["o_copied"], 1)

                        def pair(p, it, j):
                            for d, (qt, kb) in enumerate(steps):
                                act.wait_ge(s["weighted"], p * NS + d + 1)
                                for k in range(4):
                                    at = first_query(qt, kb + k // 2)
                                    n = 4 * d + k
                                    act.wait_ge(s["scored"], p * NT + n + 1)
                                    nc.scalar.activation(prob[:, n % PRING, at:BT], psum[:, S0 + (j * NT + n) % SBANKS, at:BT],
                                                         ACT.Exp).then_inc(s["exp"], 1)
                                if d >= 1 and ended(d - 1) is not None:
                                    copy_out(p, ended(d - 1))
                                elif d == 0 and not first(p):
                                    copy_out(p - 1, NB - 1)
                                if d == LEAD and not last_pair(p):
                                    copy_max(p + 1)

                        act.sem_inc(s["exp"], SBANKS)
                        act.sem_inc(s["o_copied"], CREDIT)
                        act.wait_ge(s["max_turned"], 1)
                        nc.scalar.activation(max_rows[:, :], psum[0:2 * NPART * TT, X0, 0:HALF].bitcast(BF16), ACT.Copy).then_inc(s["max_rows"], 1)
                        loop(nc.scalar, pair)
                        copy_out(NPAIR - 1, NB - 1)

                    @block.vector
                    def _(dve):
                        def maxima(p, b, m, hd):
                            i, c = chunks[m]
                            n = 2 * m + hd
                            bank = M0 + (b * NM + n) % MBANKS
                            to = part_max[:, hd, i, c:c + 1]
                            if n == 0 and not first(p):
                                dve.wait_ge(s["row_max"], p)
                            if c == i // SUB:
                                diagonal = [2 * e + hd + 1 for e in range(m) if chunks[e][1] == chunks[e][0] // SUB]
                                dve.wait_ge(s["max_read"], p * NM + (diagonal[-1] if diagonal else 0) + MBANKS)
                            dve.wait_ge(s["max_scored"], p * NM + n + 1)
                            if c < i // SUB:
                                nc.vector.tensor_reduce(to, psum[:, bank, :], AX.X, ALU.max).then_inc(s["max_read"], 1)
                            else:
                                cols = P * (i % SUB + 1)
                                alone(dve, s)
                                nc.vector.tensor_tensor_reduce(out=junk[:, hd, 0:cols], in0=psum[:, bank, 0:cols],
                                                               in1=mask[:, BT - cols:BT], scale=1.0, scalar=START,
                                                               op0=ALU.add, op1=ALU.max, accum_out=to).then_inc(s["max_read"], 1)

                        def split_max(p):
                            dve.wait_ge(s["max_read"], (p + 1) * NM + MBANKS)
                            if not first(p):
                                dve.wait_ge(s["max_turned"], p)
                            nc.vector.tensor_reduce(row_max[:, :, :], part_max[:, :, :, :], AX.X, ALU.max).then_inc(s["row_max"], 1)
                            dve.wait_ge(s["row_max"], p + 1)
                            nc.vector.tensor_copy(max_parts[:, :, 0, :], row_max[:, :, :]).then_inc(s["max_step"], 1)
                            dve.wait_ge(s["max_step"], 4 * p + 1)
                            nc.vector.tensor_tensor(max_rest[:, :, :], row_max[:, :, :], max_parts[:, :, 0, :],
                                                    ALU.subtract).then_inc(s["max_step"], 1)
                            dve.wait_ge(s["max_step"], 4 * p + 2)
                            nc.vector.tensor_copy(max_parts[:, :, 1, :], max_rest[:, :, :]).then_inc(s["max_step"], 1)
                            dve.wait_ge(s["max_step"], 4 * p + 3)
                            nc.vector.tensor_tensor(max_parts[:, :, 2, :], max_rest[:, :, :], max_parts[:, :, 1, :],
                                                    ALU.subtract).then_inc(s["max_parts"], 1)
                            dve.wait_ge(s["max_parts"], p + 1)
                            dve.sem_inc(s["max_step"], 1)

                        def normalise(p, qt):
                            dve.wait_ge(s["gathered"], p * NB + qt + 1 + CREDIT)
                            got = psum[:, X0, 0:SUB * VW].rearrange("p (i c) -> p i c", c=VW)
                            dve.wait_ge(s["normed"], p * NB + qt + 1)
                            nc.vector.reciprocal(rden[:, :, :], got[:, :, 2 * HD:]).then_inc(s["rden"], 1)
                            dve.wait_ge(s["rden"], p * NB + qt + 1)
                            nc.vector.tensor_tensor(heads[:, qt * SUB:(qt + 1) * SUB, bass.ds(p * 2 * HD, 2 * HD)].rearrange(
                                                        "p i (a c) -> p i a c", c=HD),
                                                    got[:, :, 0:2 * HD].rearrange("p i (a c) -> p i a c", c=HD),
                                                    rden[:, :, :].unsqueeze(3).broadcast_to([P, SUB, 2, HD]),
                                                    ALU.mult).then_inc(s["normed"], 1)

                        def pair(p, it, j):
                            for d in range(NS):
                                if not last_pair(p):
                                    for m, hd in maxima_of(d):
                                        maxima(p + 1, (j + 1) % SB, m, hd)
                                    if d == LEAD - 1:
                                        split_max(p + 1)
                                if d >= 2 and ended(d - 2) is not None:
                                    normalise(p, ended(d - 2))
                                elif d == 1 and not first(p):
                                    normalise(p - 1, NB - 1)

                        dve.sem_inc(s["max_read"], MBANKS)
                        dve.sem_inc(s["gathered"], CREDIT)
                        dve.sem_inc(s["normed"], 1)
                        for b in range(SB):
                            last = nc.vector.memset(stack[KR:P, b, :, 1, :], -1.0)
                        last.then_inc(s["ones"], 1)
                        dve.sem_inc(s["weighted"], CREDIT)
                        dve.wait_ge(s["mask"], 12)
                        for m in range(len(chunks)):
                            for hd in range(2):
                                maxima(0, 0, m, hd)
                        split_max(0)
                        loop(nc.vector, pair)
                        normalise(NPAIR - 1, NB - 1)

        def project(s):
            with ExitStack() as st:
                tb = tensors(st, "proj")
                raw = tb("raw_o", [P, 2, H], F32)
                wfull = tb("wfull_o", [P, PL, H], F32)
                wt = tb("wt_o", [P, 2, PL, H], F32R)
                bias = tb("bias_o", [P, H], F32)
                xb = tb("xb", [P, SUB, H], F32)
                ot = tb("ot", [P, 2, 2, PL, BT], F32R)

                def loop(engine, block_steps):
                    with engine.Fori(0, NB // 2) as it:
                        block_steps(it * 2, 0, it * 2 + 1)
                        block_steps(it * 2 + 1, 1, it * -2 + 2)

                with nc.Block() as block:
                    @block.sync
                    def _(sp):
                        sp.dma_start(raw[:, :, :], Wo.rearrange("(hh p) c -> p hh c", p=P)).then_inc(s["loaded"], 16)
                        sp.dma_start(bias[:, :], bo.rearrange("(o c) -> o c", o=1).broadcast_to([P, H])).then_inc(s["loaded"], 16)

                    @block.gpsimd
                    def _(pool):
                        pool.wait_ge(s["loaded"], 32)
                        for b in range(NB):
                            tiles = x[:, b * SUB:(b + 1) * SUB, :]
                            nc.gpsimd.tensor_tensor(tiles, tiles, bias[:, :].unsqueeze(1).broadcast_to([P, SUB, H]),
                                                    ALU.add).then_inc(s["biased"], 1)

                    @block.tensor
                    def _(pe):
                        def turn(use):
                            pe.wait_ge(s["xb"], use + 1)
                            if not isinstance(use, int):
                                pe.wait_ge(s["ot_lo"], use)
                            turn_tensor(xb, 4).then_inc(s["turned"], 1)

                        def block_steps(b, k, following):
                            pe.wait_ge(s["ot_lo"], b + 1)
                            for i in range(SUB):
                                pe.wait_ge(s["added"], b * SUB + i + 1)
                                n = 0
                                for pl in range(PL):
                                    for a, c in PASSES:
                                        last = nc.tensor.matmul(psum[:, i, 0:H], ot[:, k, a, pl, i * P:(i + 1) * P],
                                                                wt[:, c, pl, :], start=(n == 0), stop=(n == 5))
                                        n += 1
                                last.then_inc(s["summed"], 1)
                                if i == 0:
                                    turn(b + 1)

                        turn(0)
                        pe.wait_ge(s["loaded"], 32)
                        for pl in range(PL):
                            for hh in range(2):
                                last = nc.tensor.transpose(psum[:, 6 + pl, hh * P:(hh + 1) * P], raw[:, hh, pl::PL], ident[:, :])
                        last.then_inc(s["wt"], 1)
                        pe.wait_ge(s["wt_lo"], 1)
                        loop(nc.tensor, block_steps)

                    @block.scalar
                    def _(act):
                        def fetch(b, use):
                            act.wait_ge(s["turned"], use + 1)
                            nc.scalar.activation(xb[:, :, :], heads[:, bass.ds(b * SUB, SUB), :], ACT.Copy).then_inc(s["xb"], 1)

                        def split(use, k):
                            act.wait_ge(s["turned"], use + 2)
                            nc.scalar.activation(ot[:, k, 0, :, :], psum[:, 4:6, :], ACT.Copy).then_inc(s["ot_hi"], 1)

                        def block_steps(b, k, following):
                            fetch(following, b + 1)
                            split(b + 1, 1 - k)

                        act.sem_inc(s["turned"], 1)
                        fetch(0, 0)
                        split(0, 0)
                        act.wait_ge(s["wt"], 1)
                        nc.scalar.activation(wfull[:, :, :], psum[:, 6:8, 0:H], ACT.Copy).then_inc(s["wfull"], 1)
                        loop(nc.scalar, block_steps)

                    @block.vector
                    def _(dve):
                        def split(use, k):
                            dve.wait_ge(s["ot_hi"], use + 1)
                            nc.vector.tensor_tensor(ot[:, k, 1, :, :], psum[:, 4:6, :], as_f32(ot[:, k, 0, :, :]),
                                                    ALU.subtract).then_inc(s["ot_lo"], 1)

                        def block_steps(b, k, following):
                            dve.wait_ge(s["biased"], b + 1)
                            for i in range(SUB):
                                dve.wait_ge(s["summed"], b * SUB + i + 1)
                                dst = x[:, bass.ds(b * SUB + i, 1), :].rearrange("p o c -> p (o c)")
                                nc.vector.tensor_tensor(dst, psum[:, i, 0:H], dst, ALU.add).then_inc(s["added"], 1)
                                if i == 1:
                                    split(b + 1, 1 - k)
                            dve.wait_ge(s["added"], (b + 2) * SUB)
                            norm_stats(b)

                        dve.sem_inc(s["added"], SUB)
                        split(0, 0)
                        dve.wait_ge(s["wfull"], 1)
                        nc.vector.tensor_copy(wt[:, 0, :, :], wfull[:, :, :]).then_inc(s["wt_hi"], 1)
                        dve.wait_ge(s["wt_hi"], 1)
                        nc.vector.tensor_tensor(wt[:, 1, :, :], wfull[:, :, :], as_f32(wt[:, 0, :, :]), ALU.subtract).then_inc(s["wt_lo"], 1)
                        loop(nc.vector, block_steps)

        NORM = "aggr var std rstd xb "
        W_SEMS = "scales x ident turned_s wide turned_c byte turned weight w_hi w_lo step value " + " ".join(f"codes{n}" for n in range(3 * NG))
        F_SEMS = NORM + "turned gu product inner_lo down added xt_hi xt_lo tanh square cubic quadratic gelu inner_hi stored"
        Q_SEMS = NORM + ("loaded wt wfull wt_hi wt_lo turned xt_hi xt_lo full unit v_sum v bias_q part_1 part_2 part_3 rest "
                         "part_out0 part_out1 part_out2 part_out3 v_out0 v_out1 v_out2 v_out3")
        A_SEMS = ("stack0 stack1 stack2 max_rows max_loaded ones scored weighted mask exp masked max_read max_scored max_parts "
                  "passed normed max_turned o_copied gathered row_max max_step rden")
        O_SEMS = "xb loaded wt wfull wt_hi wt_lo turned ot_hi ot_lo summed added biased"

        def named(phase, names):
            return {n: outer.enter_context(nc.semaphore(f"{phase}_{n}")) for n in names.split()}

        dequantise(named("dequant", W_SEMS))
        ffn("ffn1", named("ffn1", F_SEMS), False)
        qkv(named("qkv", Q_SEMS))
        attention(named("attn", A_SEMS))
        project(named("proj", O_SEMS))
        ffn("ffn2", named("ffn2", F_SEMS), True)


_INS = ["L0_attn_h", "L0_attn_Wq", "L0_attn_bq", "L0_attn_Wk", "L0_attn_bk", "L0_attn_Wv", "L0_attn_bv", "L0_attn_Wo",
        "L0_attn_bo", "L0_ffn_gate_W_packed", "L0_ffn_gate_scales", "L0_ffn_up_W_packed", "L0_ffn_up_scales",
        "L0_ffn_down_W_packed", "L0_ffn_down_scales"]


def kernel(**inputs):
    import numpy as _np
    import concourse.bacc as _bacc
    from concourse import mybir as _mybir
    from concourse.bass_utils import run_bass_kernel_spmd as _run

    nc = _bacc.Bacc("TRN2", target_bir_lowering=False, num_devices=1)
    arrays, args = {}, []
    for name in _INS:
        a = _np.ascontiguousarray(inputs[name])
        arrays[f"in_{name}"] = a
        args.append(nc.dram_tensor(f"in_{name}", a.shape, _mybir.dt.from_np(a.dtype), kind="ExternalInput").ap())
    args.append(nc.dram_tensor("out", (1, T, H), F32, kind="ExternalOutput").ap())
    build_program(nc, *args)
    r = _run(nc, [arrays], core_ids=[0])
    return r.results[0]["out"]
```
